# Optimizing a Trainium2 kernel written in Bass

```python
import numpy as np
import jax
import jax.numpy as jnp

def _softmax(x, axis=-1):
    return jax.nn.softmax(x, axis=axis)

def _gelu(x):
    return jax.nn.gelu(x, approximate=True)

def _silu(x):
    return jax.nn.silu(x)

def _sigmoid(x):
    return jax.nn.sigmoid(x)

def _layernorm(x, axis=-1, eps=1e-05):
    m = jnp.mean(x, axis=axis, keepdims=True)
    v = jnp.var(x, axis=axis, keepdims=True)
    return (x - m) / jnp.sqrt(v + eps)

def _scatter_add(tgt, idx, src, axis=0):
    return tgt.at[idx].add(src)

def _segment_sum(src, seg, n):
    return jax.ops.segment_sum(src, seg, n)
kernel_name = 'mk_adaln_d1_jaxref_r8_09df8c'

def setup_inputs(seed: int=0):
    np.random.seed(seed)
    _w = jnp.asarray

    def _L0_attn_setup():
        import jax, jax.numpy as jnp
        import numpy as np
        D_MODEL = 128
        N_HEADS = 16
        LATENT_HEADS = 8
        LATENT_DIM = 64
        N_LATENTS = 64
        WINDOW = 32
        HEAD_DIM = D_MODEL // N_HEADS
        LAT_HD = LATENT_DIM // LATENT_HEADS
        B, S = (2, 512)

        def _pool_to_latents(x):
            Bx, Sx, C = x.shape
            chunk = max(1, Sx // N_LATENTS)
            return x.reshape(Bx, N_LATENTS, chunk, C).mean(axis=2)

        def _local_window_attn(Q, K, V):
            Bx, H, Sx, D = Q.shape
            W = WINDOW
            nb = Sx // W
            Qb = Q.reshape(Bx, H, nb, W, D)
            Kp = jnp.pad(K, ((0, 0), (0, 0), (W, 0), (0, 0))).reshape(Bx, H, nb + 1, W, D)
            Vp = jnp.pad(V, ((0, 0), (0, 0), (W, 0), (0, 0))).reshape(Bx, H, nb + 1, W, D)
            Kw = jnp.concatenate([Kp[:, :, :-1], Kp[:, :, 1:]], axis=3)
            Vw = jnp.concatenate([Vp[:, :, :-1], Vp[:, :, 1:]], axis=3)
            i = jnp.arange(W)[:, None]
            j = jnp.arange(2 * W)[None, :]
            base = (j > i) & (j <= i + W)
            blk0 = (jnp.arange(nb) > 0)[:, None, None] | (j >= W)[None, :, :]
            mask = base[None, :, :] & blk0
            sc = jnp.einsum('bhnid,bhnjd->bhnij', Qb, Kw) / np.sqrt(D).astype(np.float32)
            sc = jnp.where(mask[None, None], sc, -jnp.inf)
            p = jax.nn.softmax(sc, axis=-1)
            out = jnp.einsum('bhnij,bhnjd->bhnid', p, Vw)
            return out.reshape(Bx, H, Sx, D)
        key = jax.random.key(seed)
        ks = jax.random.split(key, 11)
        std = 0.02
        w = lambda k, shp: jax.random.normal(k, shp, jnp.float32) * std
        return {'x': jax.random.normal(ks[0], (B, S, D_MODEL), jnp.float32), 'wq': w(ks[1], (D_MODEL, D_MODEL)), 'wk': w(ks[2], (D_MODEL, D_MODEL)), 'wv': w(ks[3], (D_MODEL, D_MODEL)), 'wgq': w(ks[4], (D_MODEL, LATENT_DIM)), 'wgk': w(ks[5], (D_MODEL, LATENT_DIM)), 'wgv': w(ks[6], (D_MODEL, LATENT_DIM)), 'r_out_w': w(ks[7], (LATENT_DIM, D_MODEL)), 'gate_local_w': w(ks[8], (N_HEADS, HEAD_DIM)), 'gate_remote_w': w(ks[9], (N_HEADS, HEAD_DIM)), 'w_out': w(ks[10], (D_MODEL, D_MODEL))}
    _L0_attn_in = _L0_attn_setup()

    def _L0_ffn_setup():
        import jax, jax.numpy as jnp
        import numpy as np
        B, S, H, F, E = (8, 256, 128, 512, 8)
        INIT_LAMBDA = 0.2
        key = jax.random.key(seed)
        ks = jax.random.split(key, 12)
        std = 0.02
        return {'hidden_states': jax.random.normal(ks[0], (B, S, H), jnp.float32), 'gate_w1': jax.random.normal(ks[1], (H, H), jnp.float32) * 0.01, 'gate_b1': jnp.zeros((H,), jnp.float32), 'gate_w2': jax.random.normal(ks[2], (E, H), jnp.float32) * 0.01, 'gate_b2': jnp.full((E,), INIT_LAMBDA, jnp.float32), 'W1': jax.random.normal(ks[3], (F, H), jnp.float32) * std, 'b1': jax.random.normal(ks[4], (F,), jnp.float32) * std, 'W2': jax.random.normal(ks[5], (H, F), jnp.float32) * std, 'b2': jax.random.normal(ks[6], (H,), jnp.float32) * std, 'TW1': jax.random.normal(ks[7], (E, F, H), jnp.float32) * std, 'Tb1': jax.random.normal(ks[8], (E, F), jnp.float32) * std, 'TW2': jax.random.normal(ks[9], (E, H, F), jnp.float32) * std, 'Tb2': jax.random.normal(ks[10], (E, H), jnp.float32) * std}
    _L0_ffn_in = _L0_ffn_setup()
    _L0_c = _w((lambda *s: np.random.randn(*s).astype(np.float32) * 0.05)(32, 128))
    _L0_wmod = _w((lambda *s: np.random.randn(*s).astype(np.float32) * 0.05)(128, 6 * 128) * 128 ** (-0.5))
    _d = {'L0_attn_x': _L0_attn_in['x'], 'L0_attn_wq': _L0_attn_in['wq'], 'L0_attn_wk': _L0_attn_in['wk'], 'L0_attn_wv': _L0_attn_in['wv'], 'L0_attn_wgq': _L0_attn_in['wgq'], 'L0_attn_wgk': _L0_attn_in['wgk'], 'L0_attn_wgv': _L0_attn_in['wgv'], 'L0_attn_r_out_w': _L0_attn_in['r_out_w'], 'L0_attn_gate_local_w': _L0_attn_in['gate_local_w'], 'L0_attn_gate_remote_w': _L0_attn_in['gate_remote_w'], 'L0_attn_w_out': _L0_attn_in['w_out'], 'L0_ffn_gate_w1': _L0_ffn_in['gate_w1'], 'L0_ffn_gate_b1': _L0_ffn_in['gate_b1'], 'L0_ffn_gate_w2': _L0_ffn_in['gate_w2'], 'L0_ffn_gate_b2': _L0_ffn_in['gate_b2'], 'L0_ffn_W1': _L0_ffn_in['W1'], 'L0_ffn_b1': _L0_ffn_in['b1'], 'L0_ffn_W2': _L0_ffn_in['W2'], 'L0_ffn_b2': _L0_ffn_in['b2'], 'L0_ffn_TW1': _L0_ffn_in['TW1'], 'L0_ffn_Tb1': _L0_ffn_in['Tb1'], 'L0_ffn_TW2': _L0_ffn_in['TW2'], 'L0_ffn_Tb2': _L0_ffn_in['Tb2'], 'L0_c': _L0_c, 'L0_wmod': _L0_wmod}
    _x0 = _d['L0_attn_x']
    _d['L0_attn_x'] = jax.random.normal(jax.random.fold_in(jax.random.key(seed), 1), (32, 256, 128), dtype=_x0.dtype)
    del _x0
    return _d

def reference(L0_attn_x, L0_attn_wq, L0_attn_wk, L0_attn_wv, L0_attn_wgq, L0_attn_wgk, L0_attn_wgv, L0_attn_r_out_w, L0_attn_gate_local_w, L0_attn_gate_remote_w, L0_attn_w_out, L0_ffn_gate_w1, L0_ffn_gate_b1, L0_ffn_gate_w2, L0_ffn_gate_b2, L0_ffn_W1, L0_ffn_b1, L0_ffn_W2, L0_ffn_b2, L0_ffn_TW1, L0_ffn_Tb1, L0_ffn_TW2, L0_ffn_Tb2, L0_c, L0_wmod):

    def _L0_attn_ref(x, wq, wk, wv, wgq, wgk, wgv, r_out_w, gate_local_w, gate_remote_w, w_out):
        import jax, jax.numpy as jnp
        import numpy as np
        D_MODEL = 128
        N_HEADS = 16
        LATENT_HEADS = 8
        LATENT_DIM = 64
        N_LATENTS = 64
        WINDOW = 32
        HEAD_DIM = D_MODEL // N_HEADS
        LAT_HD = LATENT_DIM // LATENT_HEADS
        B, S = (2, 512)

        def _pool_to_latents(x):
            Bx, Sx, C = x.shape
            chunk = max(1, Sx // N_LATENTS)
            return x.reshape(Bx, N_LATENTS, chunk, C).mean(axis=2)

        def _local_window_attn(Q, K, V):
            Bx, H, Sx, D = Q.shape
            W = WINDOW
            nb = Sx // W
            Qb = Q.reshape(Bx, H, nb, W, D)
            Kp = jnp.pad(K, ((0, 0), (0, 0), (W, 0), (0, 0))).reshape(Bx, H, nb + 1, W, D)
            Vp = jnp.pad(V, ((0, 0), (0, 0), (W, 0), (0, 0))).reshape(Bx, H, nb + 1, W, D)
            Kw = jnp.concatenate([Kp[:, :, :-1], Kp[:, :, 1:]], axis=3)
            Vw = jnp.concatenate([Vp[:, :, :-1], Vp[:, :, 1:]], axis=3)
            i = jnp.arange(W)[:, None]
            j = jnp.arange(2 * W)[None, :]
            base = (j > i) & (j <= i + W)
            blk0 = (jnp.arange(nb) > 0)[:, None, None] | (j >= W)[None, :, :]
            mask = base[None, :, :] & blk0
            sc = jnp.einsum('bhnid,bhnjd->bhnij', Qb, Kw) / np.sqrt(D).astype(np.float32)
            sc = jnp.where(mask[None, None], sc, -jnp.inf)
            p = jax.nn.softmax(sc, axis=-1)
            out = jnp.einsum('bhnij,bhnjd->bhnid', p, Vw)
            return out.reshape(Bx, H, Sx, D)
        Bx, Sx, _ = x.shape
        chunk = max(1, Sx // N_LATENTS)
        Q = (x @ wq).reshape(Bx, Sx, N_HEADS, HEAD_DIM).transpose(0, 2, 1, 3)
        K = (x @ wk).reshape(Bx, Sx, N_HEADS, HEAD_DIM).transpose(0, 2, 1, 3)
        V = (x @ wv).reshape(Bx, Sx, N_HEADS, HEAD_DIM).transpose(0, 2, 1, 3)
        local = _local_window_attn(Q, K, V)
        GQ = (x @ wgq).reshape(Bx, Sx, LATENT_HEADS, LAT_HD).transpose(0, 2, 1, 3)
        GK = _pool_to_latents(x @ wgk).reshape(Bx, N_LATENTS, LATENT_HEADS, LAT_HD).transpose(0, 2, 1, 3)
        GV = _pool_to_latents(x @ wgv).reshape(Bx, N_LATENTS, LATENT_HEADS, LAT_HD).transpose(0, 2, 1, 3)
        lsc = jnp.einsum('bhsd,bhnd->bhsn', GQ, GK) / np.sqrt(LAT_HD).astype(np.float32)
        lmask = jnp.arange(N_LATENTS)[None, :] <= (jnp.arange(Sx) // chunk)[:, None]
        lsc = jnp.where(lmask[None, None], lsc, -jnp.inf)
        lp = jax.nn.softmax(lsc, axis=-1)
        rem = jnp.einsum('bhsn,bhnd->bhsd', lp, GV)
        rem = rem.transpose(0, 2, 1, 3).reshape(Bx, Sx, LATENT_DIM) @ r_out_w
        rem = rem.reshape(Bx, Sx, N_HEADS, HEAD_DIM).transpose(0, 2, 1, 3)
        gl = jax.nn.sigmoid(jnp.einsum('bhsd,hd->bhs', Q, gate_local_w))[..., None]
        gr = jax.nn.sigmoid(jnp.einsum('bhsd,hd->bhs', Q, gate_remote_w))[..., None]
        out = gl * local + gr * rem
        out = out.transpose(0, 2, 1, 3).reshape(Bx, Sx, D_MODEL)
        return out @ w_out

    def _L0_ffn_ref(hidden_states, gate_w1, gate_b1, gate_w2, gate_b2, W1, b1, W2, b2, TW1, Tb1, TW2, Tb2):
        import jax, jax.numpy as jnp
        import numpy as np
        B, S, H, F, E = (8, 256, 128, 512, 8)
        INIT_LAMBDA = 0.2
        x = hidden_states
        h = jax.nn.relu(jnp.einsum('bsh,oh->bso', x, gate_w1) + gate_b1)
        g = jnp.einsum('bso,eo->bse', h, gate_w2) + gate_b2
        g = g.mean(axis=1)
        mW1 = W1 + jnp.einsum('be,efh->bfh', g, TW1)
        mb1 = b1 + g @ Tb1
        mW2 = W2 + jnp.einsum('be,ehf->bhf', g, TW2)
        mb2 = b2 + g @ Tb2
        u = jax.nn.gelu(jnp.einsum('bsh,bfh->bsf', x, mW1) + mb1[:, None, :])
        out = jnp.einsum('bsf,bhf->bsh', u, mW2) + mb2[:, None, :]
        return out
    x = L0_attn_x
    mod = (_silu(L0_c) @ L0_wmod).reshape(L0_c.shape[0], 6, 1, -1)
    sa, ca, ga, sb, cb, gb = (mod[:, 0], mod[:, 1], mod[:, 2], mod[:, 3], mod[:, 4], mod[:, 5])
    ga = (2 * (ga >= 0) - 1) * jnp.maximum(jnp.abs(ga), 0.25)
    gb = (2 * (gb >= 0) - 1) * jnp.maximum(jnp.abs(gb), 0.25)
    h = _layernorm(x, axis=-1) * (1 + ca) + sa
    x = x + ga * _L0_attn_ref(h, L0_attn_wq, L0_attn_wk, L0_attn_wv, L0_attn_wgq, L0_attn_wgk, L0_attn_wgv, L0_attn_r_out_w, L0_attn_gate_local_w, L0_attn_gate_remote_w, L0_attn_w_out)
    h = _layernorm(x, axis=-1) * (1 + cb) + sb
    x = x + gb * _L0_ffn_ref(h, L0_ffn_gate_w1, L0_ffn_gate_b1, L0_ffn_gate_w2, L0_ffn_gate_b2, L0_ffn_W1, L0_ffn_b1, L0_ffn_W2, L0_ffn_b2, L0_ffn_TW1, L0_ffn_Tb1, L0_ffn_TW2, L0_ffn_Tb2)
    return x

_drawn_inputs = setup_inputs


def setup_inputs(seed=0):
    import zlib

    import numpy as np

    out = dict(_drawn_inputs(seed))
    spreads = {'L0_ffn_gate_b1': (0.0, 0.8), 'L0_ffn_gate_b2': (0.20000000298023224, 0.6)}
    factors = {'L0_attn_wq': 8.0,
     'L0_attn_wk': 8.0,
     'L0_attn_wv': 8.0,
     'L0_attn_wgq': 8.0,
     'L0_attn_wgk': 8.0,
     'L0_attn_wgv': 8.0,
     'L0_attn_r_out_w': 8.0,
     'L0_attn_gate_local_w': 8.0,
     'L0_attn_gate_remote_w': 8.0,
     'L0_attn_w_out': 8.0,
     'L0_ffn_gate_w1': 8.0,
     'L0_ffn_gate_w2': 8.0,
     'L0_ffn_W1': 3.666,
     'L0_ffn_b1': 8.0,
     'L0_ffn_W2': 3.603,
     'L0_ffn_b2': 28.388,
     'L0_ffn_TW1': 6.364,
     'L0_ffn_Tb1': 8.0,
     'L0_ffn_TW2': 6.353,
     'L0_ffn_Tb2': 8.0,
     'L0_c': 2.987,
     'L0_wmod': 2.968}
    for name, (base, spread) in spreads.items():
        noise = np.random.default_rng([zlib.crc32(name.encode()), seed]).standard_normal(out[name].shape)
        drawn = base * np.exp(spread * noise) if base else spread * noise
        out[name] = jnp.asarray(drawn.astype(out[name].dtype))
    for name, factor in factors.items():
        out[name] = (out[name] * factor).astype(out[name].dtype)
    return out
```

```python
from contextlib import ExitStack

import numpy as np

import concourse.bass as bass
from concourse import mybir

F32 = mybir.dt.float32
BF16 = mybir.dt.bfloat16
ALU = mybir.AluOpType
ACT = mybir.ActivationFunctionType
AX = mybir.AxisListType

P = 128
D = 128
H, HD = 16, 8
LH = 8
W = 32
NL = 64
E = 8
HALF = 2 * W
BIG = 1e30


def adaln_block(nc, ins, out):
    x_d = ins["L0_attn_x"]
    B, S, _ = x_d.shape
    F = ins["L0_ffn_W1"].shape[0]
    T = S // P
    NB = S // W
    BT = P // W
    POOL = S // NL
    G = H // 4
    LG = LH // 4
    J = P // E
    GB = 8
    NG = B // GB
    FC = F // P
    KW = S + W
    SCALE = float(HD) ** -0.5
    N_KBD = 16 * H

    with ExitStack() as ctx:
        def sb(name, shape, dt=F32):
            return ctx.enter_context(nc.sbuf_tensor(name, shape, dt))

        def sem(name):
            return ctx.enter_context(nc.semaphore(name))

        SB = [ctx.enter_context(nc.psum_tensor(f"SB{k}", [P, 512], F32)) for k in range(4)]
        WB = [ctx.enter_context(nc.psum_tensor(f"WB{k}", [P, 512], F32)) for k in range(4)]

        wq, wk, wv = sb("wq", [P, D]), sb("wk", [P, D]), sb("wv", [P, D])
        wgq, wgk = sb("wgq", [P, NL]), sb("wgk", [P, NL])
        wgv = sb("wgv", [P, NL])
        r_out = sb("r_out", [NL, D])
        w_out, w_out_half = sb("w_out", [P, D]), sb("w_out_half", [P, D])
        PT = sb("PT", [P, G * 2 * S + 2 * P])
        wmod = PT[:, 0:6 * D]
        W1 = PT[:, 6 * D:6 * D + F].rearrange("p (c h) -> p c h", c=F // P)
        W2 = PT[:, 6 * D + F:6 * D + 2 * F]
        c_rows = sb("c_rows", [B, D])
        gate_col = sb("gate_col", [P, 2])
        gate_w1, gate_w1T = sb("gate_w1", [P, D]), sb("gate_w1T", [P, D])
        gate_w2, gate_w2T = sb("gate_w2", [E, D]), sb("gate_w2T", [P, E])
        gate_b1, gate_b2 = sb("gate_b1", [P, 1]), sb("gate_b2", [E, 1])
        b1_col, b2_col = sb("b1_col", [P, FC]), sb("b2_col", [P, 1])
        tb1, tb2 = sb("tb1", [E, F]), sb("tb2", [E, D])
        W1T, W2T = sb("W1T", [P, F]), sb("W2T", [P, FC, D])
        TW1 = sb("TW1", [P, F // J, D])
        TW2 = sb("TW2", [P, D // J, F])

        ident, identb = sb("ident", [P, P]), sb("identb", [P, P], BF16)
        quad = sb("quad", [P, 4])
        ones_bd = sb("ones_bd", [P, W])
        pool_bd = sb("pool_bd", [P, W])
        head = sb("head", [P, H])
        jmask = sb("jmask", [P, J])
        gate_w = [sb("gate_lw", [P, D]), sb("gate_rw", [P, D])]
        tri, tri4 = sb("tri", [P, P]), sb("tri4", [P, P])
        cur = sb("cur", [P, W])
        win = sb("win", [P, HALF])
        win_mask = [sb(f"win_mask{t}", [P, 8, HALF], BF16) for t in range(T)]
        lat_mask = sb("lat_mask", [P, 8 * W + 8 * NL], BF16)
        wait_carrier = sb("wait_carrier", [1, 1])
        minus_half, eps_row = sb("minus_half", [P, T]), sb("eps_row", [P, T])

        silu_a, silu_b, silu_c = sb("silu_a", [B, D]), sb("silu_b", [B, D]), sb("silu_c", [B, D])
        siluT = sb("siluT", [P, B])
        saT, ca1T, sbT, cb1T, gbT = (sb(n, [P, B]) for n in ("saT", "ca1T", "sbT", "cb1T", "gbT"))
        gb_sign, gb_abs = sb("gb_sign", [P, B]), sb("gb_abs", [P, B])
        ga_sign, ga_abs, ga_row = sb("ga_sign", [B, D]), sb("ga_abs", [B, D]), sb("ga_row", [B, D])
        GA = sb("GA", [P, B * D])

        x_all = sb("x_all", [P, B * S])
        h2T = sb("h2T", [P, B * S])
        hsum = sb("hsum", [P, B])

        st_a, st_d = sb("st_a", [P, T, 6]), sb("st_d", [P, T, 6])
        mv_a, mv_d = sb("mv_a", [P, T, 2]), sb("mv_d", [P, T, 2])
        ve_a, ve_d = sb("ve_a", [P, T]), sb("ve_d", [P, T])
        rstd_a, rstd_d = sb("rstd_a", [P, T]), sb("rstd_d", [P, T])
        xn_a, xn_d = sb("xn_a", [P, T, D]), sb("xn_d", [P, T, D])
        hT, hpT = sb("hT", [P, S]), sb("hpT", [P, NL])
        QT, KT = sb("QT", [P, S]), sb("KT", [P, S])
        KBD = sb("KBD", [P, H, KW])
        GQT, GKT = sb("GQT", [NL, S]), sb("GKT", [NL, NL])
        GKBD = sb("GKBD", [NL, LH, NL])
        VBD = sb("VBD", [P, NB, G, W])
        GVBD = sb("GVBD", [P, 2, LG, W])
        mx, lmx = sb("mx", [P, 4, 8]), sb("lmx", [P, T, LH])
        Pr = sb("Pr", [P, 4, 512])
        PlA, PlB = sb("PlA", [P, 1, LH * W]), sb("PlB", [P, 2, LH * W])
        PL = sb("PL", [P, LG, S + P])
        tg = sb("tg", [P, 2, S])
        rden, a_loc, a_gated = sb("rden", [P, S]), sb("a_loc", [P, S]), sb("a_gated", [P, S])
        rlden, rem_n, rem_g = sb("rlden", [NL, S]), sb("rem_n", [NL, S]), sb("rem_g", [P, S])
        attT = sb("attT", [P, S])
        y_ga = sb("y_ga", [P, S])
        relu_out = sb("relu_out", [P, S])

        gT = sb("gT", [E, B])
        e_rows = sb("e_rows", [E, E, J])
        Gd = sb("Gd", [P, NG * J * GB])
        mb1T, mb2T, gmb2T = sb("mb1T", [P, FC, B]), sb("mb2T", [P, B]), sb("gmb2T", [P, B])
        mW1 = KBD[:].rearrange("p h k -> p (h k)")[:, 0:GB * F].rearrange("p (b f) -> p b f", b=GB)
        mW2 = GA[:].rearrange("p (c b h) -> p c b h", c=FC, b=GB)
        u = [Pr[:, 2 * k:2 * k + 2, :].rearrange("p a (c s) -> p (a c) s", s=S) for k in range(2)]
        fT = [rden, a_loc]
        o_sb = [attT, y_ga]

        (w_loaded, tw_loaded, x_loaded, pool_ready, mask_ready, dve_ready, silu_exp, setup_t, setup_c,
         ga_made, ga_copied) = (sem(n) for n in (
             "w_loaded", "tw_loaded", "x_loaded", "pool_ready", "mask_ready", "dve_ready", "silu_exp",
             "setup_t", "setup_c", "ga_made", "ga_copied"))
        (stat_a, aggr_a, eps_a, rstd_a_s, xn_a_s, xT_done, hT_ready, hp_ready, qk_done, qt_ready, kt_ready,
         kbd_loaded, gqk_done, gq_ready, gkbd_ready) = (sem(n) for n in (
             "stat_a", "aggr_a", "eps_a", "rstd_a_s", "xn_a_s", "xT_done", "hT_ready", "hp_ready", "qk_done",
             "qt_ready", "kt_ready", "kbd_loaded", "gqk_done", "gq_ready", "gkbd_ready"))
        (s_ready, mx_ready, s_sub, p_ready, gv_done, gvbd_ready, v_done, vbd_ready, ls_ready, lmx_ready,
         ls_sub, pl_ready, gates_done, tg_ready) = (sem(n) for n in (
             "s_ready", "mx_ready", "s_sub", "p_ready", "gv_done", "gvbd_ready", "v_done", "vbd_ready",
             "ls_ready", "lmx_ready", "ls_sub", "pl_ready", "gates_done", "tg_ready"))
        (pt_done, pt_copied, lpt_done, lpt_copied, pv_done, rden_ready, a_ready, ag_ready, lpv_done, rlden_ready,
         remn_ready, rem_done, remg_ready, att_ready, y_done, yga_ready, x1_ready) = (sem(n) for n in (
             "pt_done", "pt_copied", "lpt_done", "lpt_copied", "pv_done", "rden_ready", "a_ready", "ag_ready",
             "lpv_done", "rlden_ready", "remn_ready", "rem_done", "remg_ready", "att_ready", "y_done",
             "yga_ready", "x1_ready"))
        (stat_d, aggr_d, eps_d, rstd_d_s, xn_d_s, x2T_done, h2T_ready, hid_done, hid_summed) = (
            sem(n) for n in ("stat_d", "aggr_d", "eps_d", "rstd_d_s", "xn_d_s", "x2T_done", "h2T_ready",
                             "hid_done", "hid_summed"))
        (g_done, g_ready, mix_done, mixed, ffn1_done, gelu_done, ffn2_done, fT_ready, fin_done, o_ready) = (
            sem(n) for n in ("g_done", "g_ready", "mix_done", "mixed", "ffn1_done", "gelu_done", "ffn2_done",
                             "fT_ready", "fin_done", "o_ready"))
        stored = [sem(f"stored{k}") for k in range(2)]

        def bc(ap, shape, *axes):
            for a in axes:
                ap = ap.unsqueeze(a)
            return ap.to_broadcast(shape)

        def at_least(eng, s, value):
            if not isinstance(value, int) or value > 0:
                eng.wait_ge(s, value)

        def bank_free(eng, it, *users):
            for lag, s, per, n in users:
                b = it - lag
                if isinstance(it, int) and not 0 <= b < B:
                    continue
                at_least(eng, s, per * b + n)
                return

        def pipeline(eng, step):
            for it in range(3):
                step(it)
            with eng.Fori(3, B) as it:
                step(it)
            for it in range(B, B + 3):
                step(it)

        def has(it, lag):
            return not isinstance(it, int) or 0 <= it - lag < B

        block = ctx.enter_context(nc.Block())

        N_W = 0
        small = [
            (wmod, ins["L0_wmod"]), (c_rows, ins["L0_c"]), (wq, ins["L0_attn_wq"]), (wk, ins["L0_attn_wk"]),
            (wv, ins["L0_attn_wv"]), (wgq, ins["L0_attn_wgq"]), (wgk, ins["L0_attn_wgk"]),
            (wgv, ins["L0_attn_wgv"]),
            (r_out, ins["L0_attn_r_out_w"]), (w_out, ins["L0_attn_w_out"]),
            (gate_col[:, 0:1], ins["L0_attn_gate_local_w"].rearrange("h (d a) -> (h d) a", a=1)),
            (gate_col[:, 1:2], ins["L0_attn_gate_remote_w"].rearrange("h (d a) -> (h d) a", a=1)),
            (gate_w1, ins["L0_ffn_gate_w1"]), (gate_w2, ins["L0_ffn_gate_w2"]),
            (gate_b1, ins["L0_ffn_gate_b1"].rearrange("(p a) -> p a", a=1)),
            (gate_b2, ins["L0_ffn_gate_b2"].rearrange("(p a) -> p a", a=1)),
            (b2_col, ins["L0_ffn_b2"].rearrange("(p a) -> p a", a=1)),
            (tb1, ins["L0_ffn_Tb1"]), (tb2, ins["L0_ffn_Tb2"]),
            (W1, ins["L0_ffn_W1"].rearrange("(c p) h -> p c h", p=P)), (W2, ins["L0_ffn_W2"]),
        ] + [(b1_col[:, c:c + 1], ins["L0_ffn_b1"][c * P:(c + 1) * P].rearrange("(p a) -> p a", a=1))
             for c in range(FC)]
        N_W = 16 * len(small)
        N_TW = 16 * 2 * E

        @block.sync
        def _(sp):
            def load_x(b):
                sp.dma_start(x_all[:, bass.ds(b * S, S)].rearrange("p (t d) -> p t d", t=T),
                             x_d[bass.ds(b, 1)].rearrange("b (t p) d -> p (b t) d", p=P)).then_inc(x_loaded, 16)

            load_x(0)
            for dst, src in small:
                sp.dma_start(dst[:] if not isinstance(dst, bass.AP) else dst, src).then_inc(w_loaded, 16)
            sp.wait_ge(pool_ready, 1)

            def step(it):
                if has(it, 0):
                    sp.wait_ge(x_loaded, 16 * (it + 1))
                    if not isinstance(it, int) or it + 1 < B:
                        load_x(it + 1)
                    sp.wait_ge(kt_ready, it + 1)
                    for h in range(H):
                        sp.dma_start(KBD[HD * h:HD * h + HD, h, W:KW],
                                     KT[HD * h:HD * h + HD, :]).then_inc(kbd_loaded, 16)

            for it in range(3):
                step(it)
            with sp.Fori(3, B - 1) as it:
                step(it)
            step(B - 1)

            with sp.Fori(0, NG) as g:
                for j in range(GB):
                    sp.wait_ge(o_ready, g * GB + (j + 1))
                    sp.dma_start(out[bass.ds(g * GB + j, 1)].rearrange("b (t p) d -> p (b t) d", p=P),
                                 o_sb[j % 2][:].rearrange("p (t d) -> p t d", t=T)).then_inc(stored[j % 2], 16)
            for k in range(2):
                sp.wait_ge(stored[k], 16 * B // 2)

        @block.gpsimd
        def _(pool):
            for e in range(E):
                pool.dma_start(TW1[J * e:J * e + J], ins["L0_ffn_TW1"][e].rearrange("(i j) h -> j i h", j=J)
                               ).then_inc(tw_loaded, 16)
                pool.dma_start(TW2[J * e:J * e + J], ins["L0_ffn_TW2"][e].rearrange("(i j) f -> j i f", j=J)
                               ).then_inc(tw_loaded, 16)
            nc.gpsimd.memset(ident[:], 0.0).then_inc(mask_ready, 1)
            nc.gpsimd.memset(tri[:], 1.0).then_inc(mask_ready, 1)
            nc.gpsimd.memset(lat_mask[:], 0.0).then_inc(mask_ready, 1)
            nc.gpsimd.memset(minus_half[:], -0.5).then_inc(mask_ready, 1)
            nc.gpsimd.memset(eps_row[:], 1e-5).then_inc(mask_ready, 1)
            pool.wait_ge(mask_ready, 5)
            nc.gpsimd.affine_select(out=ident[:], in_=ident[:], compare_op=ALU.not_equal, fill=1.0, base=0,
                                    pattern=[[-1, P]], channel_multiplier=1).then_inc(mask_ready, 1)
            nc.gpsimd.affine_select(out=tri[:], in_=tri[:], compare_op=ALU.is_ge, fill=0.0, base=0,
                                    pattern=[[-1, P]], channel_multiplier=1).then_inc(mask_ready, 1)
            l0 = lat_mask[:, 0:8 * W].rearrange("p (h n) -> p h n", h=8)
            l1 = lat_mask[:, 8 * W:].rearrange("p (h n) -> p h n", h=8)
            nc.gpsimd.affine_select(out=l0, in_=l0, compare_op=ALU.is_ge, fill=-BIG, base=0,
                                    pattern=[[0, 8], [-POOL, W]], channel_multiplier=1).then_inc(mask_ready, 1)
            nc.gpsimd.affine_select(out=l1, in_=l1, compare_op=ALU.is_ge, fill=-BIG, base=P,
                                    pattern=[[0, 8], [-POOL, NL]], channel_multiplier=1).then_inc(mask_ready, 1)
            nc.gpsimd.memset(KBD[:], 0.0).then_inc(pool_ready, 1)

            def inv_std(b, aggr, mv, ve, eps, rstd, rstd_s):
                pool.wait_ge(aggr, T * (b + 1))
                nc.gpsimd.tensor_tensor(ve[:], mv[:, :, 1], eps_row[:], ALU.add).then_inc(eps, 1)
                pool.wait_ge(eps, b + 1)
                nc.gpsimd.tensor_tensor(rstd[:], ve[:], minus_half[:], ALU.pow).then_inc(rstd_s, 1)

            def step(it):
                if has(it, 0):
                    inv_std(it, aggr_a, mv_a, ve_a, eps_a, rstd_a, rstd_a_s)
                if has(it, 3):
                    inv_std(it - 3, aggr_d, mv_d, ve_d, eps_d, rstd_d, rstd_d_s)
                if has(it, 2):
                    b = it - 2
                    pool.wait_ge(ag_ready, b + 1)
                    pool.wait_ge(remg_ready, b + 1)
                    at_least(pool, y_done, b)
                    nc.gpsimd.tensor_tensor(attT[:], a_gated[:], rem_g[:], ALU.add).then_inc(att_ready, 1)
                    pool.wait_ge(yga_ready, b + 1)
                    xb = x_all[:, bass.ds(b * S, S)]
                    nc.gpsimd.tensor_tensor(xb, xb, y_ga[:], ALU.add).then_inc(x1_ready, 1)
                if has(it, 0):
                    pool.wait_ge(gq_ready, 2 * (it + 1))
                    if isinstance(it, int) and it == 0:
                        pool.wait_ge(dve_ready, 1)
                    nc.gpsimd.tensor_tensor(GKBD[:], bc(GKT[:], [NL, LH, NL], 1),
                                            bc(head[0:NL, 0:LH], [NL, LH, NL], 2), ALU.mult).then_inc(gkbd_ready, 1)

            pipeline(pool, step)

        @block.scalar
        def _(act):
            act.wait_ge(w_loaded, N_W)
            nc.scalar.activation(silu_a[:], c_rows[:], ACT.Exp, scale=-1.0).then_inc(silu_exp, 1)

            act.wait_ge(setup_t, 1)
            nc.scalar.copy(W1T[:], SB[0][:]).then_inc(setup_c, 1)
            act.wait_ge(setup_t, 2)
            nc.scalar.copy(W2T[:].rearrange("p c h -> p (c h)"), SB[1][:]).then_inc(setup_c, 1)
            act.wait_ge(setup_t, 3)
            nc.scalar.copy(gate_w1T[:], SB[2][:, 0:P]).then_inc(setup_c, 1)
            nc.scalar.copy(gate_w2T[:], SB[2][:, P:P + E]).then_inc(setup_c, 1)
            act.wait_ge(setup_t, 4)
            nc.scalar.copy(siluT[:], SB[3][:, 0:B]).then_inc(setup_c, 1)
            for n in range(B // 4):
                act.wait_ge(ga_made, n + 1)
                nc.scalar.copy(GA[:, n * 512:(n + 1) * 512], WB[2 + n % 2][:]).then_inc(ga_copied, 1)

            def step(it):
                if has(it, 2):
                    b = it - 2
                    for q in range(4):
                        act.wait_ge(pt_done, 4 * b + (q + 1))
                        t, gp = divmod(q, 2)
                        dst = PT[:, gp * 4 * S:(gp + 1) * 4 * S].rearrange("p (k s) -> p k s", s=S)[:, :, t * P:(t + 1) * P]
                        nc.scalar.copy(dst, WB[(1 + q) % 4][:].rearrange("p (k s) -> p k s", s=P)).then_inc(pt_copied, 1)
                    act.wait_ge(lpt_done, 2 * b + 1)
                    nc.scalar.copy(PL[:, :, 0:S].rearrange("p g (t s) -> p t g s", t=T),
                                   WB[1][:].rearrange("p (t g s) -> p t g s", t=T, g=LG)).then_inc(lpt_copied, 1)
                    act.wait_ge(lpt_done, 2 * b + 2)
                    nc.scalar.copy(PL[:, :, S:S + P],
                                   WB[2][:, 0:2 * P].rearrange("p (g s) -> p g s", g=LG)).then_inc(lpt_copied, 1)
                if has(it, 1):
                    b = it - 1
                    for k in range(4):
                        act.wait_ge(s_sub, 4 * b + (k + 1))
                        nc.scalar.activation(Pr[:, k, :], Pr[:, k, :], ACT.Exp).then_inc(p_ready, 1)
                if has(it, 0):
                    act.wait_ge(xT_done, it + 1)
                    at_least(act, hp_ready, it)
                    if isinstance(it, int) and it == 0:
                        act.wait_ge(dve_ready, 2)
                    nc.scalar.activation(hT[:], SB[0][:, 0:S], ACT.Identity, scale=ca1T[:, bass.ds(it, 1)],
                                         bias=saT[:, bass.ds(it, 1)]).then_inc(hT_ready, 1)
                if has(it, 3):
                    b = it - 3
                    act.wait_ge(x2T_done, b + 1)
                    nc.scalar.activation(h2T[:, bass.ds(b * S, S)], WB[1][:, 0:S], ACT.Identity,
                                         scale=cb1T[:, bass.ds(b, 1)], bias=sbT[:, bass.ds(b, 1)]).then_inc(h2T_ready, 1)
                if has(it, 0):
                    act.wait_ge(qk_done, it + 1)
                    at_least(act, kbd_loaded, N_KBD * it)
                    nc.scalar.activation(KT[:], WB[0][:, S:2 * S], ACT.Copy, scale=SCALE).then_inc(kt_ready, 1)
                    nc.scalar.copy(QT[:], WB[0][:, 0:S]).then_inc(qt_ready, 1)
                if has(it, 1):
                    b = it - 1
                    act.wait_ge(gates_done, b + 1)
                    at_least(act, ag_ready, b)
                    at_least(act, remg_ready, b)
                    nc.scalar.activation(tg[:].rearrange("p k s -> p (k s)"), WB[3][:], ACT.Tanh, scale=0.5
                                         ).then_inc(tg_ready, 1)
                if has(it, 3):
                    b = it - 3
                    act.wait_ge(hid_done, b + 1)
                    at_least(act, hid_summed, b)
                    nc.scalar.activation(relu_out[:], WB[1][:, S:2 * S], ACT.Relu, bias=gate_b1[:],
                                         accum_out=hsum[:, bass.ds(b, 1)]).then_inc(hid_summed, 1)
                if has(it, 1):
                    b = it - 1
                    for t, pl in ((0, PlA), (1, PlB)):
                        act.wait_ge(ls_sub, 2 * b + (t + 1))
                        nc.scalar.activation(pl[:], pl[:], ACT.Exp).then_inc(pl_ready, 1)
                if has(it, 0):
                    act.wait_ge(gqk_done, it + 1)
                    nc.scalar.activation(GQT[:], WB[2][0:NL, 0:S], ACT.Copy, scale=SCALE / POOL).then_inc(gq_ready, 1)
                    nc.scalar.copy(GKT[:], WB[2][0:NL, S:S + NL]).then_inc(gq_ready, 1)

            pipeline(act, step)

            with act.Fori(0, NG) as g:
                for j in range(GB):
                    act.wait_ge(ffn1_done, g * GB + (j + 1))
                    if j >= 2:
                        act.wait_ge(ffn2_done, g * GB + (j - 1))
                    for c in range(FC):
                        nc.scalar.activation(u[j % 2][:, c, :], WB[2 * (j % 2) + c // 2][:, (c % 2) * S:(c % 2 + 1) * S],
                                             ACT.Gelu_apprx_tanh, bias=mb1T[:, c, bass.ds(g * GB + j, 1)]
                                             ).then_inc(gelu_done, 1)

        @block.vector
        def _(dve):
            n = [0]
            chain = sem("setup_chain")

            def then(ins_):
                n[0] += 1
                ins_.then_inc(chain, 1)
                dve.wait_ge(chain, n[0])

            dve.wait_ge(mask_ready, 9)
            then(nc.vector.tensor_copy(identb[:], ident[:]))
            then(nc.vector.tensor_reduce(quad[:], ident[:].rearrange("p (h c) -> p h c", h=4), AX.X, ALU.add))
            then(nc.vector.tensor_reduce(head[:], ident[:].rearrange("p (h d) -> p h d", d=HD), AX.X, ALU.add))
            then(nc.vector.tensor_reduce(jmask[:], ident[:].rearrange("p (e j) -> p j e", j=J), AX.X, ALU.add))
            then(nc.vector.tensor_copy(ones_bd[:].rearrange("p (h d) -> p h d", h=4), bc(quad[:], [P, 4, HD], 2)))
            then(nc.vector.tensor_scalar(pool_bd[:], ones_bd[:], 1.0 / POOL, None, ALU.mult))
            then(nc.vector.tensor_tensor(tri4[:].rearrange("p (k c) -> p k c", k=4), tri[:].rearrange("p (k c) -> p k c", k=4),
                                         bc(quad[:], [P, 4, W], 2), ALU.mult))
            then(nc.vector.tensor_reduce(cur[:], tri4[:].rearrange("p (k c) -> p c k", k=4), AX.X, ALU.add))
            then(nc.vector.tensor_scalar(win[:, 0:W], cur[:], -BIG, None, ALU.mult))
            then(nc.vector.tensor_scalar(win[:, W:HALF], cur[:], 1.0, BIG, ALU.subtract, ALU.mult))
            for t in range(T):
                then(nc.vector.tensor_copy(win_mask[t][:], bc(win[:], [P, 8, HALF], 1)))
            then(nc.vector.memset(win_mask[0][0:W, :, 0:W], -BIG))
            then(nc.vector.tensor_copy(e_rows[:], bc(ident[0:E, 0:E], [E, E, J], 2)))
            dve.wait_ge(w_loaded, N_W)
            for k in range(2):
                then(nc.vector.tensor_scalar(gate_w[k][:].rearrange("p (h d) -> p h d", d=HD), bc(head[:], [P, H, HD], 2),
                                             gate_col[:, k:k + 1], None, ALU.mult))
            nc.vector.tensor_scalar(w_out_half[:], w_out[:], 0.5, None, ALU.mult).then_inc(dve_ready, 1)
            dve.wait_ge(silu_exp, 1)
            then(nc.vector.tensor_scalar(silu_b[:], silu_a[:], 1.0, None, ALU.add))
            then(nc.vector.reciprocal(silu_c[:], silu_b[:]))
            nc.vector.tensor_tensor(silu_b[:], silu_c[:], c_rows[:], ALU.mult).then_inc(silu_exp, 1)
            dve.wait_ge(setup_t, 5)
            mod = [WB[0][:, k * B:(k + 1) * B] for k in range(6)]
            for dst, k, add in ((saT, 0, 0.0), (ca1T, 1, 1.0), (sbT, 3, 0.0), (cb1T, 4, 1.0)):
                then(nc.vector.tensor_scalar(dst[:], mod[k], add, None, ALU.add))
            for g, sign, size, dst in ((WB[1][0:B, 0:D], ga_sign, ga_abs, ga_row), (mod[5], gb_sign, gb_abs, gbT)):
                then(nc.vector.tensor_scalar(sign[:], g, 0.0, 2.0, ALU.is_ge, ALU.mult))
                then(nc.vector.scalar_tensor_tensor(size[:], sign[:], -1.0, g, ALU.add, ALU.mult))
                then(nc.vector.tensor_scalar(size[:], size[:], 0.25, None, ALU.max))
                then(nc.vector.scalar_tensor_tensor(dst[:], sign[:], -1.0, size[:], ALU.add, ALU.mult))
            nc.vector.memset(wait_carrier[:], 0.0).then_inc(dve_ready, 1)

            def stats(src, st, stat, mv, aggr, b, last_use):
                for t in range(T):
                    nc.vector.bn_stats(st[:, t, :], src[:, t * D:(t + 1) * D]).then_inc(stat, 1)
                dve.wait_ge(stat, T * (b + 1))
                nc.vector.memset(wait_carrier[:], 0.0)
                for t in range(T):
                    nc.vector.bn_aggr(mv[:, t, :], st[:, t, :]).then_inc(aggr, 1)

            def block_diagonal(dst, psum, mask, n):
                return nc.vector.tensor_tensor(
                    dst[:].rearrange("p k g (h d) -> p (k g) h d", h=4),
                    bc(psum.rearrange("p (n d) -> p n d", n=n), [P, n, 4, HD], 2),
                    bc(mask[:].rearrange("p (h d) -> p h d", h=4), [P, n, 4, HD], 1), ALU.mult)

            def normed(src, mv, rstd, xn, xn_s):
                for t in range(T):
                    nc.vector.tensor_scalar(xn[:, t, :], src[:, t * D:(t + 1) * D], mv[:, t, 0:1], rstd[:, t:t + 1],
                                            ALU.subtract, ALU.mult).then_inc(xn_s, 1)

            def step(it):
                if has(it, 0):
                    dve.wait_ge(x_loaded, 16 * (it + 1))
                    stats(x_all[:, bass.ds(it * S, S)], st_a, stat_a, mv_a, aggr_a, it, xn_a_s)
                if has(it, 3):
                    dve.wait_ge(x1_ready, it - 3 + 1)
                    stats(x_all[:, bass.ds((it - 3) * S, S)], st_d, stat_d, mv_d, aggr_d, it - 3, xn_d_s)
                if has(it, 1):
                    b = it - 1
                    for k in range(4):
                        dve.wait_ge(s_ready, 4 * b + (k + 1))
                        s_k = SB[k][:].rearrange("p (h j) -> p h j", h=8)
                        nc.vector.tensor_reduce(mx[:, k, :], s_k, AX.X, ALU.max).then_inc(mx_ready, 1)
                        dve.wait_ge(mx_ready, 4 * b + (k + 1))
                        at_least(dve, pt_done, 4 * b + (k - 3))
                        nc.vector.tensor_tensor(Pr[:, k, :].rearrange("p (w h c) -> p h w c", w=2, h=8),
                                                SB[k][:].rearrange("p (h w c) -> p h w c", w=2, h=8),
                                                bc(mx[:, k, :], [P, 8, 2, W], 2, 2), ALU.subtract).then_inc(s_sub, 1)
                if has(it, 0):
                    dve.wait_ge(rstd_a_s, it + 1)
                    at_least(dve, xT_done, it)
                    normed(x_all[:, bass.ds(it * S, S)], mv_a, rstd_a, xn_a, xn_a_s)
                if has(it, 3):
                    b = it - 3
                    dve.wait_ge(rstd_d_s, b + 1)
                    at_least(dve, x2T_done, b)
                    normed(x_all[:, bass.ds(b * S, S)], mv_d, rstd_d, xn_d, xn_d_s)
                if has(it, 1):
                    b = it - 1
                    dve.wait_ge(gv_done, b + 1)
                    block_diagonal(GVBD, WB[1][:, 0:2 * LG * HD], pool_bd, 2 * LG).then_inc(gvbd_ready, 1)
                    dve.wait_ge(v_done, b + 1)
                    block_diagonal(VBD, SB[0][:, 0:NB * G * HD], ones_bd, NB * G).then_inc(vbd_ready, 1)
                if has(it, 2):
                    b = it - 2
                    dve.wait_ge(pv_done, b + 1)
                    nc.vector.reciprocal(rden[:], WB[3][:, S:2 * S]).then_inc(rden_ready, 1)
                    dve.wait_ge(rden_ready, b + 1)
                    nc.vector.tensor_tensor(a_loc[:], WB[3][:, 0:S], rden[:], ALU.mult).then_inc(a_ready, 1)
                    dve.wait_ge(lpv_done, b + 1)
                    nc.vector.reciprocal(rlden[:], WB[0][0:NL, S:2 * S]).then_inc(rlden_ready, 1)
                    dve.wait_ge(rlden_ready, b + 1)
                    at_least(dve, rem_done, b)
                    nc.vector.tensor_tensor(rem_n[:], WB[0][0:NL, 0:S], rlden[:], ALU.mult).then_inc(remn_ready, 1)
                    dve.wait_ge(a_ready, b + 1)
                    dve.wait_ge(tg_ready, b + 1)
                    at_least(dve, att_ready, b)
                    nc.vector.scalar_tensor_tensor(a_gated[:], tg[:, 0, :], 1.0, a_loc[:], ALU.add, ALU.mult).then_inc(ag_ready, 1)
                if has(it, 1):
                    b = it - 1
                    for t, pl, m in ((0, PlA, W), (1, PlB, NL)):
                        dve.wait_ge(ls_ready, 2 * b + (t + 1))
                        s_t = SB[2 + t][:, 0:LH * m].rearrange("p (h j) -> p h j", h=LH)
                        nc.vector.tensor_reduce(lmx[:, t, :], s_t, AX.X, ALU.max).then_inc(lmx_ready, 1)
                        dve.wait_ge(lmx_ready, 2 * b + (t + 1))
                        at_least(dve, lpt_done, 2 * b)
                        nc.vector.tensor_tensor(pl[:].rearrange("p k (h n) -> p h k n", n=W),
                                                s_t.rearrange("p h (k n) -> p h k n", n=W),
                                                bc(lmx[:, t, :], [P, LH, m // W, W], 2, 2), ALU.subtract).then_inc(ls_sub, 1)
                if has(it, 0):
                    dve.wait_ge(hT_ready, it + 1)
                    nc.vector.tensor_reduce(hpT[:], hT[:].rearrange("p (n k) -> p n k", k=POOL), AX.X, ALU.add
                                            ).then_inc(hp_ready, 1)
                if has(it, 2):
                    b = it - 2
                    dve.wait_ge(rem_done, b + 1)
                    at_least(dve, att_ready, b)
                    nc.vector.scalar_tensor_tensor(rem_g[:], tg[:, 1, :], 1.0, WB[2][:, 0:S], ALU.add, ALU.mult
                                                   ).then_inc(remg_ready, 1)
                    dve.wait_ge(y_done, b + 1)
                    at_least(dve, x1_ready, b)
                    nc.vector.tensor_tensor(y_ga[:].rearrange("p (t d) -> p t d", t=T),
                                            SB[1][:, 0:S].rearrange("p (t d) -> p t d", t=T),
                                            bc(GA[:, bass.ds(b * D, D)], [P, T, D], 1), ALU.mult).then_inc(yga_ready, 1)

            dve.wait_ge(ga_copied, B // 4)
            pipeline(dve, step)

            dve.wait_ge(g_done, 1)
            nc.vector.tensor_scalar(gT[:], SB[0][0:E, 0:B], 1.0 / S, gate_b2[:], ALU.mult, ALU.add).then_inc(g_ready, 1)
            dve.wait_ge(g_done, 2)
            for g in range(NG):
                nc.vector.tensor_tensor(Gd[:, g * J * GB:(g + 1) * J * GB].rearrange("p (j b) -> p j b", j=J),
                                        bc(SB[1][:, g * GB:(g + 1) * GB], [P, J, GB], 1), bc(jmask[:], [P, J, GB], 2),
                                        ALU.mult).then_inc(g_ready, 1)
            dve.wait_ge(g_done, 3)
            for c in range(FC):
                nc.vector.tensor_scalar(mb1T[:, c, :], SB[2][:, c * B:(c + 1) * B], b1_col[:, c:c + 1], None, ALU.add
                                        ).then_inc(g_ready, 1)
            then(nc.vector.tensor_scalar(mb2T[:], SB[2][:, FC * B:(FC + 1) * B], b2_col[:], None, ALU.add))
            nc.vector.tensor_tensor(gmb2T[:], mb2T[:], gbT[:], ALU.mult).then_inc(g_ready, 1)

            banks = SB + WB
            dve.wait_ge(g_ready, 1 + NG + FC + 1)
            with dve.Fori(0, NG) as g:
                for m in range(16):
                    dve.wait_ge(mix_done, g * 16 + (m + 1))
                    psum = banks[m % 8][:].rearrange("p (r b) -> p r b", b=GB)
                    if m < 8:
                        dst = mW1[:, :, m * 64:(m + 1) * 64].rearrange("p b r -> p r b")
                        base = W1T[:, m * 64:(m + 1) * 64]
                    else:
                        c, half = divmod(m - 8, 2)
                        dst = mW2[:, c, :, half * 64:half * 64 + 64].rearrange("p b r -> p r b")
                        base = W2T[:, c, half * 64:half * 64 + 64]
                    nc.vector.tensor_tensor(dst, psum, bc(base, [P, 64, GB], 2), ALU.add).then_inc(mixed, 1)

                def out_row(j):
                    dve.wait_ge(fin_done, g * GB + (j + 1))
                    if j >= 2:
                        dve.wait_ge(stored[j % 2], g * (16 * GB // 2) + 16 * (j // 2))
                    nc.vector.tensor_tensor(o_sb[j % 2][:], SB[2 + j % 2][:, 0:S], x_all[:, bass.ds((g * GB + j) * S, S)],
                                            ALU.add).then_inc(o_ready, 1)

                for j in range(GB):
                    dve.wait_ge(ffn2_done, g * GB + (j + 1))
                    if j >= 2:
                        dve.wait_ge(fin_done, g * GB + (j - 1))
                    nc.vector.tensor_scalar(fT[j % 2][:], SB[j % 2][:, 0:S], gbT[:, bass.ds(g * GB + j, 1)],
                                            gmb2T[:, bass.ds(g * GB + j, 1)], ALU.mult, ALU.add).then_inc(fT_ready, 1)
                    if j >= 1:
                        out_row(j - 1)
                out_row(GB - 1)
                for k in range(2):
                    dve.wait_ge(stored[k], (g + 1) * (16 * GB // 2))

        @block.tensor
        def _(pe):
            mm = nc.tensor.matmul
            pe.wait_ge(mask_ready, 9)
            pe.wait_ge(w_loaded, N_W)
            for c in range(FC):
                last = nc.tensor.transpose(SB[0][:, c * P:(c + 1) * P], W1[:, c, :], ident[:])
            last.then_inc(setup_t, 1)
            for c in range(FC):
                last = nc.tensor.transpose(SB[1][:, c * P:(c + 1) * P], W2[:, c * P:(c + 1) * P], ident[:])
            last.then_inc(setup_t, 1)
            nc.tensor.transpose(SB[2][:, 0:P], gate_w1[:], ident[:])
            nc.tensor.transpose(SB[2][:, P:P + E], gate_w2[:], ident[0:E, 0:E]).then_inc(setup_t, 1)
            pe.wait_ge(silu_exp, 2)
            nc.tensor.transpose(SB[3][:, 0:B], silu_b[:], ident[0:B, 0:B]).then_inc(setup_t, 1)
            pe.wait_ge(setup_c, 5)
            for k in range(6):
                mm(WB[0][:, k * B:(k + 1) * B], wmod[:, k * D:(k + 1) * D], siluT[:], start=True, stop=True)
            mm(WB[1][0:B, 0:D], siluT[:], wmod[:, 2 * D:3 * D], start=True, stop=True).then_inc(setup_t, 1)
            pe.wait_ge(dve_ready, 2)
            for n in range(B // 4):
                at_least(pe, ga_copied, n - 1)
                for k in range(4):
                    b = 4 * n + k
                    last = mm(WB[2 + n % 2][:, k * D:(k + 1) * D], ident[0:B, b:b + 1].to_broadcast([B, P]), ga_row[:],
                              start=True, stop=True)
                last.then_inc(ga_made, 1)
            pe.wait_ge(ga_copied, B // 4)

            def scores(it):
                b = it - 1
                pe.wait_ge(qt_ready, b + 1)
                for k in range(4):
                    t, hh = divmod(k, 2)
                    if k == 0:
                        bank_free(pe, it, (1, hT_ready, 1, 1))
                    if k == 1:
                        bank_free(pe, it, (3, yga_ready, 1, 1), (2, s_sub, 4, 2))
                    if k >= 2:
                        bank_free(pe, it, (2, ls_sub, 2, k - 1))
                    mm(SB[k][:], identb[:], win_mask[t][:].rearrange("p h j -> p (h j)"), start=True, stop=False,
                       skip_group_check=True)
                    if k == 0:
                        pe.wait_ge(kbd_loaded, N_KBD * (b + 1))
                    for q in range(BT):
                        blk = BT * t + q
                        last = mm(SB[k][W * q:W * q + W, :].rearrange("p (h j) -> p h j", h=8),
                                  QT[:, W * blk:W * blk + W],
                                  KBD[:, 8 * hh:8 * hh + 8, W * blk:W * blk + HALF], start=False, stop=True,
                                  skip_group_check=True)
                    last.then_inc(s_ready, 1)

            def probs_T(it):
                b = it - 2
                users = [((4, hid_summed, 1, 1), (2, gvbd_ready, 1, 1)),
                         ((1, gq_ready, 2, 2), (3, remg_ready, 1, 1)),
                         ((2, tg_ready, 1, 1),),
                         ((1, qt_ready, 1, 1), (3, remn_ready, 1, 1))]
                for q in range(4):
                    pe.wait_ge(p_ready, 4 * b + (q + 1))
                    bank_free(pe, it, *users[q])
                    for k in range(4):
                        g2, before = divmod(k, 2)
                        o = ((1 - before) * 8 + 4 * g2) * W
                        src = Pr[:, q, o:o + P]
                        last = nc.tensor.transpose(WB[(1 + q) % 4][:, k * P:(k + 1) * P], src, ident[:])
                    last.then_inc(pt_done, 1)

            def latent_T(it):
                b = it - 2
                pe.wait_ge(pl_ready, 2 * (b + 1))
                bank_free(pe, it, (2, pt_copied, 4, 1))
                for g in range(LG):
                    nc.tensor.transpose(WB[1][:, g * P:(g + 1) * P], PlA[:, 0, g * P:(g + 1) * P], ident[:])
                for g in range(LG):
                    last = nc.tensor.transpose(WB[1][:, (2 + g) * P:(3 + g) * P], PlB[:, 0, g * P:(g + 1) * P], ident[:])
                last.then_inc(lpt_done, 1)
                bank_free(pe, it, (2, pt_copied, 4, 2))
                for g in range(LG):
                    last = nc.tensor.transpose(WB[2][:, g * P:(g + 1) * P], PlB[:, 1, g * P:(g + 1) * P], ident[:])
                last.then_inc(lpt_done, 1)

            def values(it):
                b = it - 2
                pe.wait_ge(pt_copied, 4 * (b + 1))
                pe.wait_ge(vbd_ready, b + 1)
                for kb in range(NB):
                    for g in range(G):
                        o = g * 2 * S + kb * W
                        if kb < NB - 1:
                            pt = PT[:, o:o + 2 * (S + W)].rearrange("p (k s) -> p k s", k=2)[:, :, 0:W]
                            dst = WB[3][W * g:W * g + W, kb * W:kb * W + HALF].rearrange("p (k s) -> p k s", k=2)
                        else:
                            pt, dst = PT[:, o:o + W], WB[3][W * g:W * g + W, kb * W:kb * W + W]
                        mm(dst, VBD[:, kb, g, :], pt, start=(kb == 0), stop=(kb == NB - 1), skip_group_check=True)
                for before in range(2):
                    for g in range(G):
                        o = (2 * g + before) * S
                        last = mm(WB[3][W * g:W * g + W, S:2 * S], ones_bd[:], PT[:, o:o + S], start=False,
                                  stop=(before == 1), skip_group_check=True)
                last.then_inc(pv_done, 1)

            def latent_values(it):
                b = it - 2
                pe.wait_ge(lpt_copied, 2 * (b + 1))
                pe.wait_ge(gvbd_ready, b + 1)
                for den in range(2):
                    for k in range(2):
                        for g in range(LG):
                            o = WB[0][W * g:W * g + W, den * S:(den + 1) * S]
                            last = mm(o if k == 0 else o[:, P:S], ones_bd[:] if den else GVBD[:, k, g, :],
                                      PL[:, g, 0:S] if k == 0 else PL[:, g, S:S + P], start=(den == 0 and k == 0),
                                      stop=(k == 1), skip_group_check=True)
                last.then_inc(lpv_done, 1)

            def value_rows(it):
                b = it - 1
                bank_free(pe, it, (2, lpt_copied, 2, 1))
                wgv_h = wgv[:].rearrange("p (g h d) -> p g h d", g=LG, h=4)
                for k in range(2):
                    for h in range(4):
                        last = mm(WB[1][W * h:W * h + W, k * 16:(k + 1) * 16].rearrange("p (g d) -> p g d", g=LG),
                                  hpT[:, k * W:(k + 1) * W], wgv_h[:, :, h, :], start=True, stop=True)
                last.then_inc(gv_done, 1)
                pe.wait_ge(s_sub, 4 * b + 1)
                wv_h = wv[:].rearrange("p (g h d) -> p g h d", g=G, h=4)
                for kb in range(NB):
                    for h in range(4):
                        last = mm(SB[0][W * h:W * h + W, kb * W:(kb + 1) * W].rearrange("p (g d) -> p g d", g=G),
                                  hT[:, kb * W:(kb + 1) * W], wv_h[:, :, h, :], start=True, stop=True)
                last.then_inc(v_done, 1)

            def latent_scores(it):
                b = it - 1
                pe.wait_ge(gq_ready, 2 * (b + 1))
                pe.wait_ge(gkbd_ready, b + 1)
                for t, m, o in ((0, W, 0), (1, NL, 8 * W)):
                    pe.wait_ge(s_sub, 4 * b + (2 + t + 1))
                    mm(SB[2 + t][:, 0:8 * m], identb[:], lat_mask[:, o:o + 8 * m], start=True, stop=False,
                       skip_group_check=True)
                    mm(SB[2 + t][:, 0:8 * m].rearrange("p (h j) -> p h j", h=8), GQT[:, t * P:(t + 1) * P],
                       GKBD[:, :, 0:m], start=False, stop=True, skip_group_check=True).then_inc(ls_ready, 1)

            def step(it):
                if has(it, 2):
                    probs_T(it)
                if has(it, 1):
                    scores(it)
                if has(it, 2):
                    latent_T(it)
                    values(it)
                    latent_values(it)
                if has(it, 1):
                    value_rows(it)
                    latent_scores(it)
                if has(it, 0):
                    pe.wait_ge(xn_a_s, T * (it + 1))
                    bank_free(pe, it, (1, vbd_ready, 1, 1))
                    for t in range(T):
                        last = nc.tensor.transpose(SB[0][:, t * P:(t + 1) * P], xn_a[:, t, :], ident[:])
                    last.then_inc(xT_done, 1)
                if has(it, 3):
                    pe.wait_ge(xn_d_s, T * (it - 3 + 1))
                    bank_free(pe, it, (1, gvbd_ready, 1, 1), (2, lpt_copied, 2, 1), (4, hid_summed, 1, 1))
                    for t in range(T):
                        last = nc.tensor.transpose(WB[1][:, t * P:(t + 1) * P], xn_d[:, t, :], ident[:])
                    last.then_inc(x2T_done, 1)
                if has(it, 1):
                    bank_free(pe, it, (2, a_ready, 1, 1))
                    for k in range(2):
                        last = mm(WB[3][:, k * S:(k + 1) * S], gate_w[k][:], QT[:], start=True, stop=True)
                    last.then_inc(gates_done, 1)
                if has(it, 0):
                    pe.wait_ge(hT_ready, it + 1)
                    bank_free(pe, it, (2, remn_ready, 1, 1), (1, qt_ready, 1, 1))
                    mm(WB[0][:, 0:S], wq[:], hT[:], start=True, stop=True)
                    mm(WB[0][:, S:2 * S], wk[:], hT[:], start=True, stop=True).then_inc(qk_done, 1)
                if has(it, 2):
                    pe.wait_ge(remn_ready, it - 2 + 1)
                    bank_free(pe, it, (2, lpt_copied, 2, 2))
                    mm(WB[2][:, 0:S], r_out[:], rem_n[:], start=True, stop=True).then_inc(rem_done, 1)
                if has(it, 3):
                    b = it - 3
                    pe.wait_ge(h2T_ready, b + 1)
                    mm(WB[1][:, S:2 * S], gate_w1T[:], h2T[:, bass.ds(b * S, S)], start=True, stop=True
                       ).then_inc(hid_done, 1)
                if has(it, 2):
                    b = it - 2
                    pe.wait_ge(att_ready, b + 1)
                    bank_free(pe, it, (1, s_sub, 4, 2), (3, yga_ready, 1, 1))
                    for t in range(T):
                        last = mm(SB[1][:, t * P:(t + 1) * P], attT[:, t * P:(t + 1) * P], w_out_half[:], start=True,
                                  stop=True)
                    last.then_inc(y_done, 1)
                if has(it, 0):
                    pe.wait_ge(hp_ready, it + 1)
                    bank_free(pe, it, (2, remg_ready, 1, 1), (1, gq_ready, 2, 2))
                    mm(WB[2][0:NL, 0:S], wgq[:], hT[:], start=True, stop=True)
                    mm(WB[2][0:NL, S:S + NL], wgk[:], hpT[:], start=True, stop=True).then_inc(gqk_done, 1)

            pipeline(pe, step)

            pe.wait_ge(hid_summed, B)
            pe.wait_ge(yga_ready, B)
            mm(SB[0][0:E, 0:B], gate_w2T[:], hsum[:], start=True, stop=True).then_inc(g_done, 1)
            pe.wait_ge(g_ready, 1)
            mm(SB[1][:, 0:B], e_rows[:].rearrange("e k j -> e (k j)"), gT[:], start=True, stop=True).then_inc(g_done, 1)
            for c in range(FC):
                mm(SB[2][:, c * B:(c + 1) * B], tb1[:, c * P:(c + 1) * P], gT[:], start=True, stop=True)
            mm(SB[2][:, FC * B:(FC + 1) * B], tb2[:], gT[:], start=True, stop=True).then_inc(g_done, 1)

            banks = SB + WB
            pe.wait_ge(tw_loaded, N_TW)
            pe.wait_ge(g_ready, 1 + NG + FC + 1)
            with pe.Fori(0, NG) as g:
                for m in range(16):
                    if m >= 8:
                        pe.wait_ge(mixed, g * 16 + (m - 7))
                    for k in range(4):
                        if m < 8:
                            lhsT = TW1[:, 4 * m + k, :]
                        else:
                            c, half = divmod(m - 8, 2)
                            lhsT = TW2[:, 4 * half + k, c * P:(c + 1) * P]
                        last = mm(banks[m % 8][:, k * P:(k + 1) * P], lhsT, Gd[:, bass.ds(g * (J * GB), J * GB)],
                                  start=True, stop=True)
                    last.then_inc(mix_done, 1)

                def ffn1(j):
                    if j < 2:
                        pe.wait_ge(mixed, g * 16 + 16)
                    else:
                        pe.wait_ge(gelu_done, g * (FC * GB) + FC * (j - 1))
                    for c in range(FC):
                        last = mm(WB[2 * (j % 2) + c // 2][:, (c % 2) * S:(c % 2 + 1) * S], mW1[:, j, c * P:(c + 1) * P],
                                  h2T[:, bass.ds((g * GB + j) * S, S)], start=True, stop=True)
                    last.then_inc(ffn1_done, 1)

                def final_T(j):
                    pe.wait_ge(fT_ready, g * GB + (j + 1))
                    if j >= 2:
                        pe.wait_ge(o_ready, g * GB + (j - 1))
                    for t in range(T):
                        last = nc.tensor.transpose(SB[2 + j % 2][:, t * P:(t + 1) * P], fT[j % 2][:, t * P:(t + 1) * P], ident[:])
                    last.then_inc(fin_done, 1)

                ffn1(0)
                ffn1(1)
                for j in range(GB):
                    pe.wait_ge(gelu_done, g * (FC * GB) + FC * (j + 1))
                    if j >= 2:
                        pe.wait_ge(fT_ready, g * GB + (j - 1))
                    for c in range(FC):
                        last = mm(SB[j % 2][:, 0:S], mW2[:, c, j, :], u[j % 2][:, c, :], start=(c == 0), stop=(c == FC - 1))
                    last.then_inc(ffn2_done, 1)
                    if j + 2 < GB:
                        ffn1(j + 2)
                    if j >= 1:
                        final_T(j - 1)
                final_T(GB - 1)
                pe.wait_ge(o_ready, (g + 1) * GB)


_NAMES = ["L0_attn_x", "L0_attn_wq", "L0_attn_wk", "L0_attn_wv", "L0_attn_wgq", "L0_attn_wgk", "L0_attn_wgv",
          "L0_attn_r_out_w", "L0_attn_gate_local_w", "L0_attn_gate_remote_w", "L0_attn_w_out", "L0_ffn_gate_w1",
          "L0_ffn_gate_b1", "L0_ffn_gate_w2", "L0_ffn_gate_b2", "L0_ffn_W1", "L0_ffn_b1", "L0_ffn_W2", "L0_ffn_b2",
          "L0_ffn_TW1", "L0_ffn_Tb1", "L0_ffn_TW2", "L0_ffn_Tb2", "L0_c", "L0_wmod"]


def kernel(**inputs):
    import concourse.bacc as bacc
    from concourse.bass_utils import run_bass_kernel_spmd

    nc = bacc.Bacc("TRN2", target_bir_lowering=False, num_devices=1)
    arrays, ins = {}, {}
    for name in _NAMES:
        a = np.ascontiguousarray(inputs[name])
        arrays[f"in_{name}"] = a
        ins[name] = nc.dram_tensor(f"in_{name}", a.shape, mybir.dt.from_np(a.dtype), kind="ExternalInput").ap()
    x = arrays["in_L0_attn_x"]
    out = nc.dram_tensor("out_x", x.shape, mybir.dt.from_np(x.dtype), kind="ExternalOutput").ap()
    adaln_block(nc, ins, out)
    r = run_bass_kernel_spmd(nc, [arrays], core_ids=[0])
    return r.results[0]["out_x"]
```

```python
from contextlib import ExitStack

import numpy as np

import concourse.bass as bass
from concourse import mybir

F32 = mybir.dt.float32
BF16 = mybir.dt.bfloat16
ALU = mybir.AluOpType
ACT = mybir.ActivationFunctionType
AX = mybir.AxisListType

P = 128
D = 128
H, HD = 16, 8
LH = 8
W = 32
NL = 64
E = 8
HALF = 2 * W
BIG = 1e30


def adaln_block(nc, ins, out):
    x_d = ins["L0_attn_x"]
    B, S, _ = x_d.shape
    F = ins["L0_ffn_W1"].shape[0]
    T = S // P
    NB = S // W
    BT = P // W
    POOL = S // NL
    G = H // 4
    LG = LH // 4
    J = P // E
    GB = 8
    NG = B // GB
    FC = F // P
    KW = S + W
    SCALE = float(HD) ** -0.5
    N_KBD = 16 * G

    with ExitStack() as ctx:
        def sb(name, shape, dt=F32):
            return ctx.enter_context(nc.sbuf_tensor(name, shape, dt))

        def sem(name):
            return ctx.enter_context(nc.semaphore(name))

        SB = [ctx.enter_context(nc.psum_tensor(f"SB{k}", [P, 512], F32)) for k in range(4)]
        WB = [ctx.enter_context(nc.psum_tensor(f"WB{k}", [P, 512], F32)) for k in range(4)]

        wq, wk, wv = sb("wq", [P, D]), sb("wk", [P, D]), sb("wv", [P, D])
        wgq, wgk = sb("wgq", [P, NL]), sb("wgk", [P, NL])
        wgv = sb("wgv", [P, NL])
        r_out = sb("r_out", [P, T, D])
        w_out_half = sb("w_out_half", [P, D])
        Pr = sb("Pr", [P, 4, 512])
        early = Pr[:].rearrange("p k n -> p (k n)").rearrange("p (k n) -> p k n", n=P)
        tri, tri4, gate_w1, w_out = (early[:, k, :] for k in range(4))
        gate_w2 = early[0:E, 4, :]
        c_rows, silu_a, silu_b, silu_c, ga_sign, ga_abs, ga_row = (early[0:B, k, :] for k in range(5, 12))
        gb_sign, gb_abs = early[:, 12, 0:B], early[:, 12, B:2 * B]
        PT = sb("PT", [P, G * 2 * S + 2 * P])
        wmod = PT[:, 0:6 * D]
        W1 = PT[:, 6 * D:6 * D + F].rearrange("p (c h) -> p c h", c=F // P)
        W2 = PT[:, 6 * D + F:6 * D + 2 * F]
        gate_col = sb("gate_col", [P, 2])
        gate_w1T, gate_w2T = sb("gate_w1T", [P, D]), sb("gate_w2T", [P, E])
        gate_b1, gate_b2 = sb("gate_b1", [P, 1]), sb("gate_b2", [E, 1])
        b1_col, b2_col = sb("b1_col", [P, FC]), sb("b2_col", [P, 1])
        tb1, tb2 = sb("tb1", [E, F]), sb("tb2", [E, D])
        W1T, W2T = sb("W1T", [P, F]), sb("W2T", [P, FC, D])
        TW1 = sb("TW1", [P, F // J, D])
        TW2 = sb("TW2", [P, D // J, F])

        ident, identb = sb("ident", [P, P]), sb("identb", [P, P], BF16)
        quad = sb("quad", [P, 4])
        ones_bd = sb("ones_bd", [P, W])
        pool_bd = sb("pool_bd", [P, W])
        head = sb("head", [P, H])
        jmask = sb("jmask", [P, J])
        gate_w = [sb("gate_lw", [P, D]), sb("gate_rw", [P, D])]
        cur = sb("cur", [P, W])
        win = sb("win", [P, HALF])
        win_mask = [sb(f"win_mask{t}", [P, 8, HALF], BF16) for t in range(T)]
        lat_mask = sb("lat_mask", [P, 8 * W + 8 * NL], BF16)
        wait_carrier = sb("wait_carrier", [1, 1])
        minus_half, eps_row = sb("minus_half", [P, T]), sb("eps_row", [P, T])

        siluT = sb("siluT", [P, B])
        saT, ca1T, sbT, cb1T, gbT = (sb(n, [P, B]) for n in ("saT", "ca1T", "sbT", "cb1T", "gbT"))
        GA = sb("GA", [P, B * D])

        x_all = sb("x_all", [P, B * S])
        h2T = sb("h2T", [P, B * S])
        hsum = sb("hsum", [P, B])

        st_a, st_d = sb("st_a", [P, T, 6]), sb("st_d", [P, T, 6])
        mv_a, mv_d = sb("mv_a", [P, T, 2]), sb("mv_d", [P, T, 2])
        ve_a, ve_d = sb("ve_a", [P, T]), sb("ve_d", [P, T])
        rstd_a, rstd_d = sb("rstd_a", [P, T]), sb("rstd_d", [P, T])
        xn_a, xn_d = sb("xn_a", [P, T, D]), sb("xn_d", [P, T, D])
        hT, hpT = sb("hT", [P, S]), sb("hpT", [P, NL])
        QT = sb("QT", [P, S])
        KM = sb("KM", [P, 4, S])
        bd_scale = sb("bd_scale", [P, 4])
        KBD = sb("KBD", [P, H, KW])
        GQT, GKT = sb("GQT", [NL, S]), sb("GKT", [NL, NL])
        GKBD = sb("GKBD", [NL, LH, NL])
        VBD = sb("VBD", [P, NB, G, W])
        GVBD = sb("GVBD", [P, 2, LG, W])
        mx, lmx = sb("mx", [P, 4, 8]), sb("lmx", [P, T, LH])
        PlA, PlB = sb("PlA", [P, 1, LH * W]), sb("PlB", [P, 2, LH * W])
        PL = sb("PL", [P, LG, S + P])
        tg = sb("tg", [P, 2, S])
        rden, a_loc, a_gated = sb("rden", [P, S]), sb("a_loc", [P, S]), sb("a_gated", [P, S])
        rlden, rem_n = sb("rlden", [P, P]), sb("rem_n", [P, P])
        rem_g = sb("rem_g", [P, S])
        attT = sb("attT", [P, S])
        y_ga = sb("y_ga", [P, S])

        gT = sb("gT", [E, B])
        e_rows = sb("e_rows", [E, E, J])
        Gd = sb("Gd", [P, NG * J * GB])
        mb1T, mb2T, gmb2T = sb("mb1T", [P, FC, B]), sb("mb2T", [P, B]), sb("gmb2T", [P, B])
        mW1 = KBD[:].rearrange("p h k -> p (h k)")[:, 0:GB * F].rearrange("p (b f) -> p b f", b=GB)
        mW2 = GA[:].rearrange("p (c b h) -> p c b h", c=FC, b=GB)
        u = [Pr[:, 2 * k:2 * k + 2, :].rearrange("p a (c s) -> p (a c) s", s=S) for k in range(2)]
        fT = [rden, a_loc]
        o_sb = [attT, y_ga]

        (w_loaded, tw_loaded, x_loaded, pool_ready, mask_ready, dve_ready, silu_exp, setup_t, setup_c,
         ga_made, ga_copied) = (sem(n) for n in (
             "w_loaded", "tw_loaded", "x_loaded", "pool_ready", "mask_ready", "dve_ready", "silu_exp",
             "setup_t", "setup_c", "ga_made", "ga_copied"))
        (stat_a, aggr_a, eps_a, rstd_a_s, xn_a_s, xT_done, hT_ready, hp_ready, qk_done, qt_ready, km_ready,
         kbd_loaded, gqk_done, gq_ready, gkbd_ready) = (sem(n) for n in (
             "stat_a", "aggr_a", "eps_a", "rstd_a_s", "xn_a_s", "xT_done", "hT_ready", "hp_ready", "qk_done",
             "qt_ready", "km_ready", "kbd_loaded", "gqk_done", "gq_ready", "gkbd_ready"))
        (s_ready, mx_ready, s_sub, p_ready, gv_done, gvbd_ready, v_done, vbd_ready, ls_ready, lmx_ready,
         ls_sub, pl_ready, gates_done, tg_ready) = (sem(n) for n in (
             "s_ready", "mx_ready", "s_sub", "p_ready", "gv_done", "gvbd_ready", "v_done", "vbd_ready",
             "ls_ready", "lmx_ready", "ls_sub", "pl_ready", "gates_done", "tg_ready"))
        (pt_done, pt_copied, lpt_done, lpt_copied, pv_done, rden_ready, a_ready, ag_ready, lpv_done, rlden_ready,
         remn_ready, rem_done, remg_ready, att_ready, y_done, yga_ready, x1_ready) = (sem(n) for n in (
             "pt_done", "pt_copied", "lpt_done", "lpt_copied", "pv_done", "rden_ready", "a_ready", "ag_ready",
             "lpv_done", "rlden_ready", "remn_ready", "rem_done", "remg_ready", "att_ready", "y_done",
             "yga_ready", "x1_ready"))
        (stat_d, aggr_d, eps_d, rstd_d_s, xn_d_s, x2T_done, h2T_ready, hid_done, hid_summed) = (
            sem(n) for n in ("stat_d", "aggr_d", "eps_d", "rstd_d_s", "xn_d_s", "x2T_done", "h2T_ready",
                             "hid_done", "hid_summed"))
        (g_done, g_ready, mix_done, mixed, ffn1_done, gelu_done, ffn2_done, fT_ready, fin_done, o_ready) = (
            sem(n) for n in ("g_done", "g_ready", "mix_done", "mixed", "ffn1_done", "gelu_done", "ffn2_done",
                             "fT_ready", "fin_done", "o_ready"))
        stored = [sem(f"stored{k}") for k in range(2)]

        def bc(ap, shape, *axes):
            for a in axes:
                ap = ap.unsqueeze(a)
            return ap.to_broadcast(shape)

        def at_least(eng, s, value):
            if not isinstance(value, int) or value > 0:
                eng.wait_ge(s, value)

        def bank_free(eng, it, *users):
            for lag, s, per, n in users:
                b = it - lag
                if isinstance(it, int) and not 0 <= b < B:
                    continue
                at_least(eng, s, per * b + n)
                return

        def pipeline(eng, step):
            for it in range(4):
                step(it)
            with eng.Fori(4, B) as it:
                step(it)
            for it in range(B, B + 4):
                step(it)

        def has(it, lag):
            return not isinstance(it, int) or 0 <= it - lag < B

        PT_BANKS = [WB[3], WB[1], SB[2], SB[3]]

        block = ctx.enter_context(nc.Block())

        N_W = 0
        small = [
            (wmod, ins["L0_wmod"]), (c_rows, ins["L0_c"]), (wq, ins["L0_attn_wq"]), (wk, ins["L0_attn_wk"]),
            (wv, ins["L0_attn_wv"]), (wgq, ins["L0_attn_wgq"]), (wgk, ins["L0_attn_wgk"]),
            (wgv, ins["L0_attn_wgv"]),
            (r_out[0:NL, 0, :], ins["L0_attn_r_out_w"]), (r_out[NL:P, 1, :], ins["L0_attn_r_out_w"]),
            (w_out, ins["L0_attn_w_out"]),
            (gate_col[:, 0:1], ins["L0_attn_gate_local_w"].rearrange("h (d a) -> (h d) a", a=1)),
            (gate_col[:, 1:2], ins["L0_attn_gate_remote_w"].rearrange("h (d a) -> (h d) a", a=1)),
            (gate_w1, ins["L0_ffn_gate_w1"]), (gate_w2, ins["L0_ffn_gate_w2"]),
            (gate_b1, ins["L0_ffn_gate_b1"].rearrange("(p a) -> p a", a=1)),
            (gate_b2, ins["L0_ffn_gate_b2"].rearrange("(p a) -> p a", a=1)),
            (b2_col, ins["L0_ffn_b2"].rearrange("(p a) -> p a", a=1)),
            (tb1, ins["L0_ffn_Tb1"]), (tb2, ins["L0_ffn_Tb2"]),
            (W1, ins["L0_ffn_W1"].rearrange("(c p) h -> p c h", p=P)), (W2, ins["L0_ffn_W2"]),
        ] + [(b1_col[:, c:c + 1], ins["L0_ffn_b1"][c * P:(c + 1) * P].rearrange("(p a) -> p a", a=1))
             for c in range(FC)]
        N_W = 16 * len(small)
        N_TW = 16 * 2 * E

        @block.sync
        def _(sp):
            def load_x(b):
                sp.dma_start(x_all[:, bass.ds(b * S, S)].rearrange("p (t d) -> p t d", t=T),
                             x_d[bass.ds(b, 1)].rearrange("b (t p) d -> p (b t) d", p=P)).then_inc(x_loaded, 16)

            load_x(0)
            sp.wait_ge(pool_ready, 1)
            for dst, src in small:
                sp.dma_start(dst[:] if not isinstance(dst, bass.AP) else dst, src).then_inc(w_loaded, 16)
            sp.wait_ge(pool_ready, 2)

            def step(it):
                if has(it, 0):
                    sp.wait_ge(x_loaded, 16 * (it + 1))
                    if not isinstance(it, int) or it + 1 < B:
                        load_x(it + 1)
                    sp.wait_ge(km_ready, it + 1)
                    for g in range(G):
                        sp.dma_start(KBD[W * g:W * g + W, 4 * g:4 * g + 4, W:KW], KM[W * g:W * g + W]
                                     ).then_inc(kbd_loaded, 16)

            for it in range(3):
                step(it)
            with sp.Fori(3, B - 1) as it:
                step(it)
            step(B - 1)

            with sp.Fori(0, NG) as g:
                for j in range(GB):
                    sp.wait_ge(o_ready, g * GB + (j + 1))
                    sp.dma_start(out[bass.ds(g * GB + j, 1)].rearrange("b (t p) d -> p (b t) d", p=P),
                                 o_sb[j % 2][:].rearrange("p (t d) -> p t d", t=T)).then_inc(stored[j % 2], 16)
            for k in range(2):
                sp.wait_ge(stored[k], 16 * B // 2)

        @block.gpsimd
        def _(pool):
            nc.gpsimd.memset(r_out[:], 0.0).then_inc(pool_ready, 1)
            for e in range(E):
                pool.dma_start(TW1[J * e:J * e + J], ins["L0_ffn_TW1"][e].rearrange("(i j) h -> j i h", j=J)
                               ).then_inc(tw_loaded, 16)
                pool.dma_start(TW2[J * e:J * e + J], ins["L0_ffn_TW2"][e].rearrange("(i j) f -> j i f", j=J)
                               ).then_inc(tw_loaded, 16)
            nc.gpsimd.memset(ident[:], 0.0).then_inc(mask_ready, 1)
            nc.gpsimd.memset(tri[:], 1.0).then_inc(mask_ready, 1)
            nc.gpsimd.memset(lat_mask[:], 0.0).then_inc(mask_ready, 1)
            nc.gpsimd.memset(minus_half[:], -0.5).then_inc(mask_ready, 1)
            nc.gpsimd.memset(eps_row[:], 1e-5).then_inc(mask_ready, 1)
            pool.wait_ge(mask_ready, 5)
            nc.gpsimd.affine_select(out=ident[:], in_=ident[:], compare_op=ALU.not_equal, fill=1.0, base=0,
                                    pattern=[[-1, P]], channel_multiplier=1).then_inc(mask_ready, 1)
            nc.gpsimd.affine_select(out=tri[:], in_=tri[:], compare_op=ALU.is_ge, fill=0.0, base=0,
                                    pattern=[[-1, P]], channel_multiplier=1).then_inc(mask_ready, 1)
            l0 = lat_mask[:, 0:8 * W].rearrange("p (h n) -> p h n", h=8)
            l1 = lat_mask[:, 8 * W:].rearrange("p (h n) -> p h n", h=8)
            nc.gpsimd.affine_select(out=l0, in_=l0, compare_op=ALU.is_ge, fill=-BIG, base=0,
                                    pattern=[[0, 8], [-POOL, W]], channel_multiplier=1).then_inc(mask_ready, 1)
            nc.gpsimd.affine_select(out=l1, in_=l1, compare_op=ALU.is_ge, fill=-BIG, base=P,
                                    pattern=[[0, 8], [-POOL, NL]], channel_multiplier=1).then_inc(mask_ready, 1)
            nc.gpsimd.memset(KBD[:], 0.0).then_inc(pool_ready, 1)

            def inv_std(b, aggr, mv, ve, eps, rstd, rstd_s):
                pool.wait_ge(aggr, T * (b + 1))
                nc.gpsimd.tensor_tensor(ve[:], mv[:, :, 1], eps_row[:], ALU.add).then_inc(eps, 1)
                pool.wait_ge(eps, b + 1)
                nc.gpsimd.tensor_tensor(rstd[:], ve[:], minus_half[:], ALU.pow).then_inc(rstd_s, 1)

            def step(it):
                if has(it, 0):
                    inv_std(it, aggr_a, mv_a, ve_a, eps_a, rstd_a, rstd_a_s)
                if has(it, 4):
                    inv_std(it - 4, aggr_d, mv_d, ve_d, eps_d, rstd_d, rstd_d_s)
                if has(it, 3):
                    b = it - 3
                    pool.wait_ge(yga_ready, b + 1)
                    xb = x_all[:, bass.ds(b * S, S)]
                    nc.gpsimd.tensor_tensor(xb, xb, y_ga[:], ALU.add).then_inc(x1_ready, 1)
                if has(it, 2):
                    b = it - 2
                    pool.wait_ge(ag_ready, b + 1)
                    pool.wait_ge(remg_ready, b + 1)
                    at_least(pool, y_done, b)
                    nc.gpsimd.tensor_tensor(attT[:], a_gated[:], rem_g[:], ALU.add).then_inc(att_ready, 1)
                if has(it, 0):
                    pool.wait_ge(gq_ready, 2 * (it + 1))
                    if isinstance(it, int) and it == 0:
                        pool.wait_ge(dve_ready, 1)
                    nc.gpsimd.tensor_tensor(GKBD[:], bc(GKT[:], [NL, LH, NL], 1),
                                            bc(head[0:NL, 0:LH], [NL, LH, NL], 2), ALU.mult).then_inc(gkbd_ready, 1)

            pipeline(pool, step)

        @block.scalar
        def _(act):
            act.wait_ge(w_loaded, N_W)
            nc.scalar.activation(silu_a[:], c_rows[:], ACT.Exp, scale=-1.0).then_inc(silu_exp, 1)

            act.wait_ge(setup_t, 1)
            nc.scalar.copy(W1T[:], SB[0][:]).then_inc(setup_c, 1)
            act.wait_ge(setup_t, 2)
            nc.scalar.copy(W2T[:].rearrange("p c h -> p (c h)"), SB[1][:]).then_inc(setup_c, 1)
            act.wait_ge(setup_t, 3)
            nc.scalar.copy(gate_w1T[:], SB[2][:, 0:P]).then_inc(setup_c, 1)
            nc.scalar.copy(gate_w2T[:], SB[2][:, P:P + E]).then_inc(setup_c, 1)
            act.wait_ge(setup_t, 4)
            nc.scalar.copy(siluT[:], SB[3][:, 0:B]).then_inc(setup_c, 1)
            for n in range(B // 4):
                act.wait_ge(ga_made, n + 1)
                nc.scalar.copy(GA[:, n * 512:(n + 1) * 512], WB[2 + n % 2][:]).then_inc(ga_copied, 1)

            def step(it):
                if has(it, 2):
                    b = it - 2
                    act.wait_ge(lpt_done, 2 * b + 1)
                    nc.scalar.copy(PL[:, :, 0:S].rearrange("p g (t s) -> p t g s", t=T),
                                   WB[1][:].rearrange("p (t g s) -> p t g s", t=T, g=LG)).then_inc(lpt_copied, 1)
                    act.wait_ge(lpt_done, 2 * b + 2)
                    nc.scalar.copy(PL[:, :, S:S + P],
                                   WB[2][:, 0:2 * P].rearrange("p (g s) -> p g s", g=LG)).then_inc(lpt_copied, 1)
                if has(it, 1):
                    b = it - 1
                    for k in range(4):
                        act.wait_ge(s_sub, 4 * b + (k + 1))
                        nc.scalar.activation(Pr[:, k, :], Pr[:, k, :], ACT.Exp).then_inc(p_ready, 1)
                if has(it, 0):
                    act.wait_ge(xT_done, it + 1)
                    at_least(act, hp_ready, it)
                    if isinstance(it, int) and it == 0:
                        act.wait_ge(dve_ready, 2)
                    nc.scalar.activation(hT[:], SB[1][:, 0:S], ACT.Identity, scale=ca1T[:, bass.ds(it, 1)],
                                         bias=saT[:, bass.ds(it, 1)]).then_inc(hT_ready, 1)
                if has(it, 1):
                    b = it - 1
                    act.wait_ge(v_done, b + 1)
                    for h in range(4):
                        nc.scalar.activation(VBD[:, :, :, h * HD:(h + 1) * HD].rearrange("p k g d -> p (k g) d"),
                                             SB[0][:, 0:NB * G * HD].rearrange("p (n d) -> p n d", d=HD), ACT.Copy,
                                             scale=quad[:, h:h + 1]).then_inc(vbd_ready, 1)
                if has(it, 0):
                    act.wait_ge(qk_done, it + 1)
                    nc.scalar.copy(QT[:], SB[2][:, 0:S]).then_inc(qt_ready, 1)
                if has(it, 1):
                    b = it - 1
                    for q in range(4):
                        act.wait_ge(pt_done, 4 * b + (q + 1))
                        t, gp = divmod(q, 2)
                        dst = PT[:, gp * 4 * S:(gp + 1) * 4 * S].rearrange("p (k s) -> p k s", s=S)[:, :, t * P:(t + 1) * P]
                        nc.scalar.copy(dst, PT_BANKS[q][:].rearrange("p (k s) -> p k s", s=P)).then_inc(pt_copied, 1)
                if has(it, 4):
                    b = it - 4
                    act.wait_ge(x2T_done, b + 1)
                    nc.scalar.activation(h2T[:, bass.ds(b * S, S)], WB[3][:, 0:S], ACT.Identity,
                                         scale=cb1T[:, bass.ds(b, 1)], bias=sbT[:, bass.ds(b, 1)]).then_inc(h2T_ready, 1)
                    act.wait_ge(hid_done, b + 1)
                    nc.scalar.activation(WB[1][:, 0:S], WB[1][:, 0:S], ACT.Relu, bias=gate_b1[:],
                                         accum_out=hsum[:, bass.ds(b, 1)]).then_inc(hid_summed, 1)
                if has(it, 1):
                    b = it - 1
                    for t, pl in ((0, PlA), (1, PlB)):
                        act.wait_ge(ls_sub, 2 * b + (t + 1))
                        nc.scalar.activation(pl[:], pl[:], ACT.Exp).then_inc(pl_ready, 1)
                if has(it, 0):
                    act.wait_ge(gqk_done, it + 1)
                    nc.scalar.activation(GQT[:], WB[3][0:NL, 0:S], ACT.Copy, scale=SCALE / POOL).then_inc(gq_ready, 1)
                    nc.scalar.copy(GKT[:], WB[3][0:NL, S:S + NL]).then_inc(gq_ready, 1)
                if has(it, 1):
                    b = it - 1
                    act.wait_ge(gates_done, b + 1)
                    at_least(act, ag_ready, b)
                    at_least(act, remg_ready, b)
                    nc.scalar.activation(tg[:].rearrange("p k s -> p (k s)"), WB[2][:], ACT.Tanh, scale=0.5
                                         ).then_inc(tg_ready, 1)

            pipeline(act, step)

            with act.Fori(0, NG) as g:
                for j in range(GB):
                    act.wait_ge(ffn1_done, g * GB + (j + 1))
                    if j >= 2:
                        act.wait_ge(ffn2_done, g * GB + (j - 1))
                    for c in range(FC):
                        nc.scalar.activation(u[j % 2][:, c, :], WB[2 * (j % 2) + c // 2][:, (c % 2) * S:(c % 2 + 1) * S],
                                             ACT.Gelu_apprx_tanh, bias=mb1T[:, c, bass.ds(g * GB + j, 1)]
                                             ).then_inc(gelu_done, 1)

        @block.vector
        def _(dve):
            n = [0]
            chain = sem("setup_chain")

            def then(ins_):
                n[0] += 1
                ins_.then_inc(chain, 1)
                dve.wait_ge(chain, n[0])

            dve.wait_ge(mask_ready, 9)
            then(nc.vector.tensor_copy(identb[:], ident[:]))
            then(nc.vector.tensor_reduce(quad[:], ident[:].rearrange("p (h c) -> p h c", h=4), AX.X, ALU.add))
            then(nc.vector.tensor_reduce(head[:], ident[:].rearrange("p (h d) -> p h d", d=HD), AX.X, ALU.add))
            then(nc.vector.tensor_reduce(bd_scale[:], head[:].rearrange("p (g h) -> p h g", h=4), AX.X, ALU.add))
            then(nc.vector.tensor_scalar(bd_scale[:], bd_scale[:], SCALE, None, ALU.mult))
            then(nc.vector.tensor_reduce(jmask[:], ident[:].rearrange("p (e j) -> p j e", j=J), AX.X, ALU.add))
            then(nc.vector.tensor_copy(ones_bd[:].rearrange("p (h d) -> p h d", h=4), bc(quad[:], [P, 4, HD], 2)))
            then(nc.vector.tensor_scalar(pool_bd[:], ones_bd[:], 1.0 / POOL, None, ALU.mult))
            then(nc.vector.tensor_tensor(tri4[:].rearrange("p (k c) -> p k c", k=4), tri[:].rearrange("p (k c) -> p k c", k=4),
                                         bc(quad[:], [P, 4, W], 2), ALU.mult))
            then(nc.vector.tensor_reduce(cur[:], tri4[:].rearrange("p (k c) -> p c k", k=4), AX.X, ALU.add))
            then(nc.vector.tensor_scalar(win[:, 0:W], cur[:], -BIG, None, ALU.mult))
            then(nc.vector.tensor_scalar(win[:, W:HALF], cur[:], 1.0, BIG, ALU.subtract, ALU.mult))
            for t in range(T):
                then(nc.vector.tensor_copy(win_mask[t][:], bc(win[:], [P, 8, HALF], 1)))
            then(nc.vector.memset(win_mask[0][0:W, :, 0:W], -BIG))
            then(nc.vector.tensor_copy(e_rows[:], bc(ident[0:E, 0:E], [E, E, J], 2)))
            dve.wait_ge(w_loaded, N_W)
            for k in range(2):
                then(nc.vector.tensor_scalar(gate_w[k][:].rearrange("p (h d) -> p h d", d=HD), bc(head[:], [P, H, HD], 2),
                                             gate_col[:, k:k + 1], None, ALU.mult))
            nc.vector.tensor_scalar(w_out_half[:], w_out[:], 0.5, None, ALU.mult).then_inc(dve_ready, 1)
            dve.wait_ge(silu_exp, 1)
            then(nc.vector.tensor_scalar(silu_b[:], silu_a[:], 1.0, None, ALU.add))
            then(nc.vector.reciprocal(silu_c[:], silu_b[:]))
            nc.vector.tensor_tensor(silu_b[:], silu_c[:], c_rows[:], ALU.mult).then_inc(silu_exp, 1)
            dve.wait_ge(setup_t, 5)
            mod = [WB[0][:, k * B:(k + 1) * B] for k in range(6)]
            for dst, k, add in ((saT, 0, 0.0), (ca1T, 1, 1.0), (sbT, 3, 0.0), (cb1T, 4, 1.0)):
                then(nc.vector.tensor_scalar(dst[:], mod[k], add, None, ALU.add))
            for g, sign, size, dst in ((WB[1][0:B, 0:D], ga_sign, ga_abs, ga_row), (mod[5], gb_sign, gb_abs, gbT)):
                then(nc.vector.tensor_scalar(sign[:], g, 0.0, 2.0, ALU.is_ge, ALU.mult))
                then(nc.vector.scalar_tensor_tensor(size[:], sign[:], -1.0, g, ALU.add, ALU.mult))
                then(nc.vector.tensor_scalar(size[:], size[:], 0.25, None, ALU.max))
                then(nc.vector.scalar_tensor_tensor(dst[:], sign[:], -1.0, size[:], ALU.add, ALU.mult))
            nc.vector.memset(wait_carrier[:], 0.0).then_inc(dve_ready, 1)

            def stats(src, st, stat, mv, aggr, b):
                for t in range(T):
                    nc.vector.bn_stats(st[:, t, :], src[:, t * D:(t + 1) * D]).then_inc(stat, 1)
                dve.wait_ge(stat, T * (b + 1))
                nc.vector.memset(wait_carrier[:], 0.0)
                for t in range(T):
                    nc.vector.bn_aggr(mv[:, t, :], st[:, t, :]).then_inc(aggr, 1)

            def normed(src, mv, rstd, xn, xn_s):
                for t in range(T):
                    nc.vector.tensor_scalar(xn[:, t, :], src[:, t * D:(t + 1) * D], mv[:, t, 0:1], rstd[:, t:t + 1],
                                            ALU.subtract, ALU.mult).then_inc(xn_s, 1)

            def step(it):
                if has(it, 0):
                    dve.wait_ge(x_loaded, 16 * (it + 1))
                    stats(x_all[:, bass.ds(it * S, S)], st_a, stat_a, mv_a, aggr_a, it)
                if has(it, 4):
                    dve.wait_ge(x1_ready, it - 4 + 1)
                    stats(x_all[:, bass.ds((it - 4) * S, S)], st_d, stat_d, mv_d, aggr_d, it - 4)
                if has(it, 1):
                    b = it - 1
                    for k in range(4):
                        dve.wait_ge(s_ready, 4 * b + (k + 1))
                        s_k = SB[k][:].rearrange("p (h j) -> p h j", h=8)
                        nc.vector.tensor_reduce(mx[:, k, :], s_k, AX.X, ALU.max).then_inc(mx_ready, 1)
                        dve.wait_ge(mx_ready, 4 * b + (k + 1))
                        at_least(dve, pt_done, 4 * b + (k - 3))
                        nc.vector.tensor_tensor(Pr[:, k, :].rearrange("p (w h c) -> p h w c", w=2, h=8),
                                                SB[k][:].rearrange("p (h w c) -> p h w c", w=2, h=8),
                                                bc(mx[:, k, :], [P, 8, 2, W], 2, 2), ALU.subtract).then_inc(s_sub, 1)
                if has(it, 0):
                    dve.wait_ge(rstd_a_s, it + 1)
                    at_least(dve, xT_done, it)
                    normed(x_all[:, bass.ds(it * S, S)], mv_a, rstd_a, xn_a, xn_a_s)
                if has(it, 3):
                    b = it - 3
                    dve.wait_ge(y_done, b + 1)
                    at_least(dve, x1_ready, b)
                    nc.vector.tensor_tensor(y_ga[:].rearrange("p (t d) -> p t d", t=T),
                                            WB[0][:, 0:S].rearrange("p (t d) -> p t d", t=T),
                                            bc(GA[:, bass.ds(b * D, D)], [P, T, D], 1), ALU.mult).then_inc(yga_ready, 1)
                if has(it, 4):
                    b = it - 4
                    dve.wait_ge(rstd_d_s, b + 1)
                    at_least(dve, x2T_done, b)
                    normed(x_all[:, bass.ds(b * S, S)], mv_d, rstd_d, xn_d, xn_d_s)
                if has(it, 2):
                    b = it - 2
                    dve.wait_ge(pv_done, b + 1)
                    nc.vector.reciprocal(rden[:], WB[3][:, S:2 * S]).then_inc(rden_ready, 1)
                if has(it, 0):
                    dve.wait_ge(hT_ready, it + 1)
                    nc.vector.tensor_reduce(hpT[:], hT[:].rearrange("p (n k) -> p n k", k=POOL), AX.X, ALU.add
                                            ).then_inc(hp_ready, 1)
                if has(it, 2):
                    b = it - 2
                    dve.wait_ge(rden_ready, b + 1)
                    nc.vector.tensor_tensor(a_loc[:], WB[3][:, 0:S], rden[:], ALU.mult).then_inc(a_ready, 1)
                if has(it, 0):
                    dve.wait_ge(qk_done, it + 1)
                    nc.vector.tensor_tensor(KM[:], bc(SB[3][:, 0:S], [P, 4, S], 1), bc(bd_scale[:], [P, 4, S], 2),
                                            ALU.mult).then_inc(km_ready, 1)
                if has(it, 2):
                    b = it - 2
                    dve.wait_ge(a_ready, b + 1)
                    dve.wait_ge(tg_ready, b + 1)
                    at_least(dve, att_ready, b)
                    nc.vector.scalar_tensor_tensor(a_gated[:], tg[:, 0, :], 1.0, a_loc[:], ALU.add, ALU.mult).then_inc(ag_ready, 1)
                    dve.wait_ge(lpv_done, b + 1)
                    nc.vector.reciprocal(rlden[:], WB[0][:, P:2 * P]).then_inc(rlden_ready, 1)
                if has(it, 1):
                    b = it - 1
                    dve.wait_ge(gv_done, b + 1)
                    at_least(dve, lpv_done, b)
                    nc.vector.tensor_tensor(GVBD[:].rearrange("p k g (h d) -> p (k g) h d", h=4),
                                            bc(WB[1][:, 0:2 * LG * HD].rearrange("p (n d) -> p n d", d=HD), [P, 2 * LG, 4, HD], 2),
                                            bc(pool_bd[:].rearrange("p (h d) -> p h d", h=4), [P, 2 * LG, 4, HD], 1),
                                            ALU.mult).then_inc(gvbd_ready, 1)
                if has(it, 2):
                    b = it - 2
                    dve.wait_ge(rlden_ready, b + 1)
                    at_least(dve, rem_done, b)
                    nc.vector.tensor_tensor(rem_n[:], WB[0][:, 0:P], rlden[:], ALU.mult).then_inc(remn_ready, 1)
                if has(it, 1):
                    b = it - 1
                    for t, pl, m in ((0, PlA, W), (1, PlB, NL)):
                        dve.wait_ge(ls_ready, 2 * b + (t + 1))
                        s_t = SB[t][:, 0:LH * m].rearrange("p (h j) -> p h j", h=LH)
                        nc.vector.tensor_reduce(lmx[:, t, :], s_t, AX.X, ALU.max).then_inc(lmx_ready, 1)
                        dve.wait_ge(lmx_ready, 2 * b + (t + 1))
                        at_least(dve, lpt_done, 2 * b)
                        nc.vector.tensor_tensor(pl[:].rearrange("p k (h n) -> p h k n", n=W),
                                                s_t.rearrange("p h (k n) -> p h k n", n=W),
                                                bc(lmx[:, t, :], [P, LH, m // W, W], 2, 2), ALU.subtract).then_inc(ls_sub, 1)
                if has(it, 2):
                    b = it - 2
                    dve.wait_ge(rem_done, b + 1)
                    at_least(dve, att_ready, b)
                    nc.vector.scalar_tensor_tensor(rem_g[:], tg[:, 1, :], 1.0, WB[0][:, 0:S], ALU.add, ALU.mult
                                                   ).then_inc(remg_ready, 1)

            dve.wait_ge(ga_copied, B // 4)
            pipeline(dve, step)

            dve.wait_ge(g_done, 1)
            nc.vector.tensor_scalar(gT[:], SB[0][0:E, 0:B], 1.0 / S, gate_b2[:], ALU.mult, ALU.add).then_inc(g_ready, 1)
            dve.wait_ge(g_done, 2)
            for g in range(NG):
                nc.vector.tensor_tensor(Gd[:, g * J * GB:(g + 1) * J * GB].rearrange("p (j b) -> p j b", j=J),
                                        bc(SB[1][:, g * GB:(g + 1) * GB], [P, J, GB], 1), bc(jmask[:], [P, J, GB], 2),
                                        ALU.mult).then_inc(g_ready, 1)
            dve.wait_ge(g_done, 3)
            for c in range(FC):
                nc.vector.tensor_scalar(mb1T[:, c, :], SB[2][:, c * B:(c + 1) * B], b1_col[:, c:c + 1], None, ALU.add
                                        ).then_inc(g_ready, 1)
            then(nc.vector.tensor_scalar(mb2T[:], SB[2][:, FC * B:(FC + 1) * B], b2_col[:], None, ALU.add))
            nc.vector.tensor_tensor(gmb2T[:], mb2T[:], gbT[:], ALU.mult).then_inc(g_ready, 1)

            banks = SB + WB
            dve.wait_ge(g_ready, 1 + NG + FC + 1)
            with dve.Fori(0, NG) as g:
                for m in range(16):
                    dve.wait_ge(mix_done, g * 16 + (m + 1))
                    psum = banks[m % 8][:].rearrange("p (r b) -> p r b", b=GB)
                    if m < 8:
                        dst = mW1[:, :, m * 64:(m + 1) * 64].rearrange("p b r -> p r b")
                        base = W1T[:, m * 64:(m + 1) * 64]
                    else:
                        c, half = divmod(m - 8, 2)
                        dst = mW2[:, c, :, half * 64:half * 64 + 64].rearrange("p b r -> p r b")
                        base = W2T[:, c, half * 64:half * 64 + 64]
                    nc.vector.tensor_tensor(dst, psum, bc(base, [P, 64, GB], 2), ALU.add).then_inc(mixed, 1)

                def out_row(j):
                    dve.wait_ge(fin_done, g * GB + (j + 1))
                    if j >= 2:
                        dve.wait_ge(stored[j % 2], g * (16 * GB // 2) + 16 * (j // 2))
                    nc.vector.tensor_tensor(o_sb[j % 2][:], SB[2 + j % 2][:, 0:S], x_all[:, bass.ds((g * GB + j) * S, S)],
                                            ALU.add).then_inc(o_ready, 1)

                for j in range(GB):
                    dve.wait_ge(ffn2_done, g * GB + (j + 1))
                    if j >= 2:
                        dve.wait_ge(fin_done, g * GB + (j - 1))
                    nc.vector.tensor_scalar(fT[j % 2][:], SB[j % 2][:, 0:S], gbT[:, bass.ds(g * GB + j, 1)],
                                            gmb2T[:, bass.ds(g * GB + j, 1)], ALU.mult, ALU.add).then_inc(fT_ready, 1)
                    if j >= 1:
                        out_row(j - 1)
                out_row(GB - 1)
                for k in range(2):
                    dve.wait_ge(stored[k], (g + 1) * (16 * GB // 2))

        @block.tensor
        def _(pe):
            mm = nc.tensor.matmul
            pe.wait_ge(mask_ready, 9)
            pe.wait_ge(w_loaded, N_W)
            for c in range(FC):
                last = nc.tensor.transpose(SB[0][:, c * P:(c + 1) * P], W1[:, c, :], ident[:])
            last.then_inc(setup_t, 1)
            for c in range(FC):
                last = nc.tensor.transpose(SB[1][:, c * P:(c + 1) * P], W2[:, c * P:(c + 1) * P], ident[:])
            last.then_inc(setup_t, 1)
            nc.tensor.transpose(SB[2][:, 0:P], gate_w1[:], ident[:])
            nc.tensor.transpose(SB[2][:, P:P + E], gate_w2[:], ident[0:E, 0:E]).then_inc(setup_t, 1)
            pe.wait_ge(silu_exp, 2)
            nc.tensor.transpose(SB[3][:, 0:B], silu_b[:], ident[0:B, 0:B]).then_inc(setup_t, 1)
            pe.wait_ge(setup_c, 5)
            for k in range(6):
                mm(WB[0][:, k * B:(k + 1) * B], wmod[:, k * D:(k + 1) * D], siluT[:], start=True, stop=True)
            mm(WB[1][0:B, 0:D], siluT[:], wmod[:, 2 * D:3 * D], start=True, stop=True).then_inc(setup_t, 1)
            pe.wait_ge(dve_ready, 2)
            for n in range(B // 4):
                at_least(pe, ga_copied, n - 1)
                for k in range(4):
                    b = 4 * n + k
                    last = mm(WB[2 + n % 2][:, k * D:(k + 1) * D], ident[0:B, b:b + 1].to_broadcast([B, P]), ga_row[:],
                              start=True, stop=True)
                last.then_inc(ga_made, 1)
            pe.wait_ge(ga_copied, B // 4)

            def scores(it):
                b = it - 1
                pe.wait_ge(qt_ready, b + 1)
                for k in range(4):
                    t, hh = divmod(k, 2)
                    if k < 2:
                        bank_free(pe, it, (2, ls_sub, 2, k + 1), (1, hT_ready, 1, 1))
                    else:
                        bank_free(pe, it, (2, pt_copied, 4, k + 1), (1, (qt_ready, km_ready)[k - 2], 1, 1))
                    mm(SB[k][:], identb[:], win_mask[t][:].rearrange("p h j -> p (h j)"), start=True, stop=False,
                       skip_group_check=True)
                    if k == 0:
                        pe.wait_ge(kbd_loaded, N_KBD * (b + 1))
                    for q in range(BT):
                        blk = BT * t + q
                        last = mm(SB[k][W * q:W * q + W, :].rearrange("p (h j) -> p h j", h=8),
                                  QT[:, W * blk:W * blk + W],
                                  KBD[:, 8 * hh:8 * hh + 8, W * blk:W * blk + HALF], start=False, stop=True,
                                  skip_group_check=True)
                    last.then_inc(s_ready, 1)

            def probs_T(it):
                b = it - 1
                users = [((2, a_ready, 1, 1),), ((1, gvbd_ready, 1, 1),),
                         ((0, qt_ready, 1, 1), (1, s_sub, 4, 3)), ((0, km_ready, 1, 1), (1, s_sub, 4, 4))]
                for q in range(4):
                    pe.wait_ge(p_ready, 4 * b + (q + 1))
                    bank_free(pe, it, *users[q])
                    for k in range(4):
                        g2, before = divmod(k, 2)
                        o = ((1 - before) * 8 + 4 * g2) * W
                        last = nc.tensor.transpose(PT_BANKS[q][:, k * P:(k + 1) * P], Pr[:, q, o:o + P], ident[:])
                    last.then_inc(pt_done, 1)

            def latent_T(it):
                b = it - 2
                pe.wait_ge(pl_ready, 2 * (b + 1))
                bank_free(pe, it, (5, hid_summed, 1, 1), (2, pt_copied, 4, 2))
                for g in range(LG):
                    nc.tensor.transpose(WB[1][:, g * P:(g + 1) * P], PlA[:, 0, g * P:(g + 1) * P], ident[:])
                for g in range(LG):
                    last = nc.tensor.transpose(WB[1][:, (2 + g) * P:(3 + g) * P], PlB[:, 0, g * P:(g + 1) * P], ident[:])
                last.then_inc(lpt_done, 1)
                bank_free(pe, it, (2, tg_ready, 1, 1))
                for g in range(LG):
                    last = nc.tensor.transpose(WB[2][:, g * P:(g + 1) * P], PlB[:, 1, g * P:(g + 1) * P], ident[:])
                last.then_inc(lpt_done, 1)

            def values(it):
                b = it - 2
                pe.wait_ge(pt_copied, 4 * (b + 1))
                pe.wait_ge(vbd_ready, 4 * (b + 1))
                bank_free(pe, it, (1, gq_ready, 2, 2), (5, h2T_ready, 1, 1), (2, pt_copied, 4, 1))
                for kb in range(NB):
                    for g in range(G):
                        o = g * 2 * S + kb * W
                        if kb < NB - 1:
                            pt = PT[:, o:o + 2 * (S + W)].rearrange("p (k s) -> p k s", k=2)[:, :, 0:W]
                            dst = WB[3][W * g:W * g + W, kb * W:kb * W + HALF].rearrange("p (k s) -> p k s", k=2)
                        else:
                            pt, dst = PT[:, o:o + W], WB[3][W * g:W * g + W, kb * W:kb * W + W]
                        mm(dst, VBD[:, kb, g, :], pt, start=(kb == 0), stop=(kb == NB - 1), skip_group_check=True)
                for before in range(2):
                    for g in range(G):
                        o = (2 * g + before) * S
                        last = mm(WB[3][W * g:W * g + W, S:2 * S], ones_bd[:], PT[:, o:o + S], start=False,
                                  stop=(before == 1), skip_group_check=True)
                last.then_inc(pv_done, 1)

            def latent_values(it):
                b = it - 2
                pe.wait_ge(lpt_copied, 2 * (b + 1))
                pe.wait_ge(gvbd_ready, b + 1)
                bank_free(pe, it, (3, yga_ready, 1, 1))
                for den in range(2):
                    for k in range(2):
                        for t in range(k, T):
                            for g in range(LG):
                                q = (LG * t + g) * W
                                last = mm(WB[0][q:q + W, den * P:(den + 1) * P], ones_bd[:] if den else GVBD[:, k, g, :],
                                          PL[:, g, (t + k) * P:(t + k + 1) * P], start=(den == 0 and k == 0),
                                          stop=(k == t), skip_group_check=True)
                last.then_inc(lpv_done, 1)

            def value_rows(it):
                b = it - 1
                bank_free(pe, it, (2, lpt_copied, 2, 1))
                wgv_h = wgv[:].rearrange("p (g h d) -> p g h d", g=LG, h=4)
                for k in range(2):
                    for h in range(4):
                        last = mm(WB[1][W * h:W * h + W, k * 16:(k + 1) * 16].rearrange("p (g d) -> p g d", g=LG),
                                  hpT[:, k * W:(k + 1) * W], wgv_h[:, :, h, :], start=True, stop=True)
                last.then_inc(gv_done, 1)
                pe.wait_ge(s_sub, 4 * b + 1)
                wv_h = wv[:].rearrange("p (g h d) -> p g h d", g=G, h=4)
                for kb in range(NB):
                    for h in range(4):
                        last = mm(SB[0][W * h:W * h + W, kb * W:(kb + 1) * W].rearrange("p (g d) -> p g d", g=G),
                                  hT[:, kb * W:(kb + 1) * W], wv_h[:, :, h, :], start=True, stop=True)
                last.then_inc(v_done, 1)

            def latent_scores(it):
                b = it - 1
                pe.wait_ge(gq_ready, 2 * (b + 1))
                pe.wait_ge(gkbd_ready, b + 1)
                for t, m, o in ((0, W, 0), (1, NL, 8 * W)):
                    if t == 0:
                        pe.wait_ge(vbd_ready, 4 * (b + 1))
                    else:
                        bank_free(pe, it, (0, hT_ready, 1, 1), (1, s_sub, 4, 2))
                    mm(SB[t][:, 0:8 * m], identb[:], lat_mask[:, o:o + 8 * m], start=True, stop=False,
                       skip_group_check=True)
                    mm(SB[t][:, 0:8 * m].rearrange("p (h j) -> p h j", h=8), GQT[:, t * P:(t + 1) * P],
                       GKBD[:, :, 0:m], start=False, stop=True, skip_group_check=True).then_inc(ls_ready, 1)

            def step(it):
                if has(it, 1):
                    scores(it)
                if has(it, 2):
                    latent_T(it)
                if has(it, 3):
                    b = it - 3
                    pe.wait_ge(att_ready, b + 1)
                    for t in range(T):
                        last = mm(WB[0][:, t * P:(t + 1) * P], attT[:, t * P:(t + 1) * P], w_out_half[:], start=True,
                                  stop=True)
                    last.then_inc(y_done, 1)
                if has(it, 2):
                    values(it)
                if has(it, 1):
                    value_rows(it)
                if has(it, 0):
                    pe.wait_ge(xn_a_s, T * (it + 1))
                    bank_free(pe, it, (1, s_sub, 4, 2))
                    for t in range(T):
                        last = nc.tensor.transpose(SB[1][:, t * P:(t + 1) * P], xn_a[:, t, :], ident[:])
                    last.then_inc(xT_done, 1)
                if has(it, 1):
                    bank_free(pe, it, (2, lpt_copied, 2, 2))
                    for k in range(2):
                        last = mm(WB[2][:, k * S:(k + 1) * S], gate_w[k][:], QT[:], start=True, stop=True)
                    last.then_inc(gates_done, 1)
                if has(it, 0):
                    pe.wait_ge(hT_ready, it + 1)
                    bank_free(pe, it, (1, s_sub, 4, 4))
                    mm(SB[3][:, 0:S], wk[:], hT[:], start=True, stop=True)
                    mm(SB[2][:, 0:S], wq[:], hT[:], start=True, stop=True).then_inc(qk_done, 1)
                if has(it, 2):
                    latent_values(it)
                if has(it, 1):
                    latent_scores(it)
                    probs_T(it)
                if has(it, 2):
                    pe.wait_ge(remn_ready, it - 2 + 1)
                    for t in range(T):
                        last = mm(WB[0][:, t * P:(t + 1) * P], r_out[:, t, :], rem_n[:], start=True, stop=True)
                    last.then_inc(rem_done, 1)
                if has(it, 4):
                    b = it - 4
                    pe.wait_ge(xn_d_s, T * (b + 1))
                    bank_free(pe, it, (1, pt_copied, 4, 1), (2, a_ready, 1, 1), (5, h2T_ready, 1, 1))
                    for t in range(T):
                        last = nc.tensor.transpose(WB[3][:, t * P:(t + 1) * P], xn_d[:, t, :], ident[:])
                    last.then_inc(x2T_done, 1)
                if has(it, 4):
                    b = it - 4
                    pe.wait_ge(h2T_ready, b + 1)
                    bank_free(pe, it, (1, pt_copied, 4, 2), (2, lpt_copied, 2, 1), (5, hid_summed, 1, 1))
                    mm(WB[1][:, 0:S], gate_w1T[:], h2T[:, bass.ds(b * S, S)], start=True, stop=True
                       ).then_inc(hid_done, 1)
                if has(it, 0):
                    pe.wait_ge(hp_ready, it + 1)
                    bank_free(pe, it, (4, h2T_ready, 1, 1), (1, pt_copied, 4, 1), (1, gq_ready, 2, 2))
                    mm(WB[3][0:NL, 0:S], wgq[:], hT[:], start=True, stop=True)
                    mm(WB[3][0:NL, S:S + NL], wgk[:], hpT[:], start=True, stop=True).then_inc(gqk_done, 1)

            pipeline(pe, step)

            pe.wait_ge(hid_summed, B)
            pe.wait_ge(yga_ready, B)
            mm(SB[0][0:E, 0:B], gate_w2T[:], hsum[:], start=True, stop=True).then_inc(g_done, 1)
            pe.wait_ge(g_ready, 1)
            mm(SB[1][:, 0:B], e_rows[:].rearrange("e k j -> e (k j)"), gT[:], start=True, stop=True).then_inc(g_done, 1)
            for c in range(FC):
                mm(SB[2][:, c * B:(c + 1) * B], tb1[:, c * P:(c + 1) * P], gT[:], start=True, stop=True)
            mm(SB[2][:, FC * B:(FC + 1) * B], tb2[:], gT[:], start=True, stop=True).then_inc(g_done, 1)

            banks = SB + WB
            pe.wait_ge(tw_loaded, N_TW)
            pe.wait_ge(g_ready, 1 + NG + FC + 1)
            with pe.Fori(0, NG) as g:
                for m in range(16):
                    if m >= 8:
                        pe.wait_ge(mixed, g * 16 + (m - 7))
                    for k in range(4):
                        if m < 8:
                            lhsT = TW1[:, 4 * m + k, :]
                        else:
                            c, half = divmod(m - 8, 2)
                            lhsT = TW2[:, 4 * half + k, c * P:(c + 1) * P]
                        last = mm(banks[m % 8][:, k * P:(k + 1) * P], lhsT, Gd[:, bass.ds(g * (J * GB), J * GB)],
                                  start=True, stop=True)
                    last.then_inc(mix_done, 1)

                def ffn1(j):
                    if j < 2:
                        pe.wait_ge(mixed, g * 16 + 16)
                    else:
                        pe.wait_ge(gelu_done, g * (FC * GB) + FC * (j - 1))
                    for c in range(FC):
                        last = mm(WB[2 * (j % 2) + c // 2][:, (c % 2) * S:(c % 2 + 1) * S], mW1[:, j, c * P:(c + 1) * P],
                                  h2T[:, bass.ds((g * GB + j) * S, S)], start=True, stop=True)
                    last.then_inc(ffn1_done, 1)

                def final_T(j):
                    pe.wait_ge(fT_ready, g * GB + (j + 1))
                    if j >= 2:
                        pe.wait_ge(o_ready, g * GB + (j - 1))
                    for t in range(T):
                        last = nc.tensor.transpose(SB[2 + j % 2][:, t * P:(t + 1) * P], fT[j % 2][:, t * P:(t + 1) * P], ident[:])
                    last.then_inc(fin_done, 1)

                ffn1(0)
                ffn1(1)
                for j in range(GB):
                    pe.wait_ge(gelu_done, g * (FC * GB) + FC * (j + 1))
                    if j >= 2:
                        pe.wait_ge(fT_ready, g * GB + (j - 1))
                    for c in range(FC):
                        last = mm(SB[j % 2][:, 0:S], mW2[:, c, j, :], u[j % 2][:, c, :], start=(c == 0), stop=(c == FC - 1))
                    last.then_inc(ffn2_done, 1)
                    if j + 2 < GB:
                        ffn1(j + 2)
                    if j >= 1:
                        final_T(j - 1)
                final_T(GB - 1)
                pe.wait_ge(o_ready, (g + 1) * GB)


_NAMES = ["L0_attn_x", "L0_attn_wq", "L0_attn_wk", "L0_attn_wv", "L0_attn_wgq", "L0_attn_wgk", "L0_attn_wgv",
          "L0_attn_r_out_w", "L0_attn_gate_local_w", "L0_attn_gate_remote_w", "L0_attn_w_out", "L0_ffn_gate_w1",
          "L0_ffn_gate_b1", "L0_ffn_gate_w2", "L0_ffn_gate_b2", "L0_ffn_W1", "L0_ffn_b1", "L0_ffn_W2", "L0_ffn_b2",
          "L0_ffn_TW1", "L0_ffn_Tb1", "L0_ffn_TW2", "L0_ffn_Tb2", "L0_c", "L0_wmod"]


def kernel(**inputs):
    import concourse.bacc as bacc
    from concourse.bass_utils import run_bass_kernel_spmd

    nc = bacc.Bacc("TRN2", target_bir_lowering=False, num_devices=1)
    arrays, ins = {}, {}
    for name in _NAMES:
        a = np.ascontiguousarray(inputs[name])
        arrays[f"in_{name}"] = a
        ins[name] = nc.dram_tensor(f"in_{name}", a.shape, mybir.dt.from_np(a.dtype), kind="ExternalInput").ap()
    x = arrays["in_L0_attn_x"]
    out = nc.dram_tensor("out_x", x.shape, mybir.dt.from_np(x.dtype), kind="ExternalOutput").ap()
    adaln_block(nc, ins, out)
    r = run_bass_kernel_spmd(nc, [arrays], core_ids=[0])
    return r.results[0]["out_x"]
```

```python
from contextlib import ExitStack

import numpy as np

import concourse.bass as bass
from concourse import mybir

F32 = mybir.dt.float32
ALU = mybir.AluOpType
ACT = mybir.ActivationFunctionType
AX = mybir.AxisListType

P = 128
D = 128
H, HD = 16, 8
LH = 8
W = 32
NL = 64
E = 8
HALF = 2 * W
BIG = 1e30


def adaln_block(nc, ins, out):
    x_d = ins["L0_attn_x"]
    B, S, _ = x_d.shape
    F = ins["L0_ffn_W1"].shape[0]
    T = S // P
    NB = S // W
    BT = P // W
    POOL = S // NL
    G = H // 4
    LG = LH // 4
    J = P // E
    GB = 8
    NG = B // GB
    FC = F // P
    KW = S + W
    SCALE = float(HD) ** -0.5
    N_KBD = 16 * G
    N_VBD = 16 * 4

    with ExitStack() as ctx:
        def sb(name, shape, dt=F32):
            return ctx.enter_context(nc.sbuf_tensor(name, shape, dt))

        def sem(name):
            return ctx.enter_context(nc.semaphore(name))

        SB = [ctx.enter_context(nc.psum_tensor(f"SB{k}", [P, 512], F32)) for k in range(4)]
        WB = [ctx.enter_context(nc.psum_tensor(f"WB{k}", [P, 512], F32)) for k in range(4)]

        wq, wk = sb("wq", [P, D]), sb("wk", [P, D])
        wv = sb("wv", [P, D])
        wgq, wgk = sb("wgq", [P, NL]), sb("wgk", [P, NL])
        wgv = sb("wgv", [P, NL])
        r_out = sb("r_out", [P, T, D])
        w_out_half = sb("w_out_half", [P, D])
        Pr = sb("Pr", [P, 4, 512])
        early = Pr[:].rearrange("p k n -> p (k n)").rearrange("p (k n) -> p k n", n=P)
        tri, tri4, w_out, wqT, wv_in, gate_cols = (early[:, k, :] for k in range(6))
        c_rows, silu_a, silu_b, silu_c, ga_sign, ga_abs = (early[0:B, k, :] for k in range(6, 12))
        gb_sign, gb_abs = early[:, 12, 0:B], early[:, 12, B:2 * B]
        PT = sb("PT", [P, G * 2 * S + 2 * P])
        PT_sum = sb("PT_sum", [P, G, S])
        wmod = PT[:, 0:6 * D]
        W1 = PT[:, 6 * D:6 * D + F].rearrange("p (c h) -> p c h", c=F // P)
        W2 = PT[:, 6 * D + F:6 * D + 2 * F]
        gate_w1, gate_w2, ga_row = (PT[0:n, 6 * D + 2 * F + k * P:6 * D + 2 * F + (k + 1) * P]
                                    for k, n in enumerate((P, E, B)))
        gate_col = sb("gate_col", [P, 2])
        gate_w1T, gate_w2T = sb("gate_w1T", [P, D]), sb("gate_w2T", [P, E])
        gate_b1, gate_b2 = sb("gate_b1", [P, 1]), sb("gate_b2", [E, 1])
        b1_col, b2_col = sb("b1_col", [P, FC]), sb("b2_col", [P, 1])
        tb1, tb2 = sb("tb1", [E, F]), sb("tb2", [E, D])
        W1T, W2T = sb("W1T", [P, F]), sb("W2T", [P, FC, D])
        TW1 = sb("TW1", [P, F // J, D])
        TW2 = sb("TW2", [P, D // J, F])

        ident = sb("ident", [P, P])
        quad = sb("quad", [P, 4])
        ones_bd = sb("ones_bd", [P, W])
        pool_bd = sb("pool_bd", [P, W])
        head = sb("head", [P, H])
        jmask = sb("jmask", [P, J])
        gate_w = sb("gate_w", [P, 2, D])
        cur = sb("cur", [P, W])
        win = sb("win", [P, HALF])
        wait_carrier = sb("wait_carrier", [1, 1])
        minus_half, eps_row = sb("minus_half", [P, T]), sb("eps_row", [P, T])

        siluT = sb("siluT", [P, B])
        saT, ca1T, sbT, cb1T, gbT = (sb(n, [P, B]) for n in ("saT", "ca1T", "sbT", "cb1T", "gbT"))
        GA = sb("GA", [P, B * D])

        x_all = sb("x_all", [P, B * S])
        h2T = sb("h2T", [P, B * S])
        hsum = sb("hsum", [P, B])

        st_a, st_d = sb("st_a", [P, T, 6]), sb("st_d", [P, T, 6])
        mv_a, mv_d = sb("mv_a", [P, T, 2]), sb("mv_d", [P, T, 2])
        ve_a, ve_d = sb("ve_a", [P, T]), sb("ve_d", [P, T])
        rstd_a, rstd_d = sb("rstd_a", [P, T]), sb("rstd_d", [P, T])
        xn_a, xn_d = sb("xn_a", [P, T, D]), sb("xn_d", [P, T, D])
        hT, hpT = sb("hT", [P, S]), sb("hpT", [P, NL])
        QT = [sb(f"QT{k}", [P, S]) for k in range(2)]
        K_ch = sb("K_ch", [P, S])
        KM = sb("KM", [P, 4, S])
        bd_scale = sb("bd_scale", [P, 4])
        KBD = sb("KBD", [P, H, KW])
        mask_rows = sb("mask_rows", [P, KW])
        GQT, GKT = sb("GQT", [P, S]), sb("GKT", [NL, NL])
        GKBD = sb("GKBD", [P, LH, NL])
        V_rows = sb("V_rows", [P, T, D])
        VBD = sb("VBD", [P, NB, 4, HD * G])
        GVBD = sb("GVBD", [P, 2, LG, W])
        mx, lmx = sb("mx", [P, 4, 8]), sb("lmx", [P, T, LH])
        PlA, PlB = sb("PlA", [P, 1, LH * W]), sb("PlB", [P, 2, LH * W])
        PL = sb("PL", [P, LG, S + P])
        tg = sb("tg", [P, 2, S])
        rden, a_loc, a_gated = sb("rden", [P, S]), sb("a_loc", [P, S]), sb("a_gated", [P, S])
        rlden, rem_n = sb("rlden", [P, P]), sb("rem_n", [P, P])
        rem_g = sb("rem_g", [P, S])
        attT = sb("attT", [P, S])
        y_ga = sb("y_ga", [P, S])

        gT = sb("gT", [E, B])
        e_rows = sb("e_rows", [E, E, J])
        Gd = sb("Gd", [P, NG * J * GB])
        mb1T, mb2T, gmb2T = sb("mb1T", [P, FC, B]), sb("mb2T", [P, B]), sb("gmb2T", [P, B])
        mW1 = KBD[:].rearrange("p h k -> p (h k)")[:, 0:GB * F].rearrange("p (b f) -> p b f", b=GB)
        mW2 = GA[:].rearrange("p (c b h) -> p c b h", c=FC, b=GB)
        u = [Pr[:, 2 * k:2 * k + 2, :].rearrange("p a (c s) -> p (a c) s", s=S) for k in range(2)]
        fT = [rden, a_loc]
        o_sb = [attT, y_ga]

        (mod_loaded, attn_loaded, w_loaded, tw_loaded, x_loaded, mask_ready, zeros_ready, head_ready, silu_exp,
         silu_ready, siluT_done, siluT_ready, mod_done, mod_ready, ga_ready, ga_stored, ga_loaded, wqT_done,
         wqT_ready, attn_w_ready, gate_w_done, gate_w_ready, masks_ready, wT_done, wT_ready) = (sem(n) for n in (
             "mod_loaded", "attn_loaded", "w_loaded", "tw_loaded", "x_loaded", "mask_ready", "zeros_ready",
             "head_ready", "silu_exp", "silu_ready", "siluT_done", "siluT_ready", "mod_done", "mod_ready",
             "ga_ready", "ga_stored", "ga_loaded", "wqT_done", "wqT_ready", "attn_w_ready", "gate_w_done",
             "gate_w_ready", "masks_ready", "wT_done", "wT_ready"))
        (stat_a, aggr_a, eps_a, rstd_a_s, xn_a_s, xT_done, hT_ready, hp_ready, qk_done, qt_ready, km_ready,
         k_ready, kbd_loaded, pts_ready, gqk_done, gq_ready, gkbd_ready) = (sem(n) for n in (
             "stat_a", "aggr_a", "eps_a", "rstd_a_s", "xn_a_s", "xT_done", "hT_ready", "hp_ready", "qk_done",
             "qt_ready", "km_ready", "k_ready", "kbd_loaded", "pts_ready", "gqk_done", "gq_ready", "gkbd_ready"))
        (s_ready, mx_ready, s_sub, p_ready, gv_done, gvbd_ready, v_done, vrows_ready, v_stored, vbd_loaded,
         masks_loaded, ls_ready, lmx_ready,
         ls_sub, pl_ready, gates_done, tg_ready) = (sem(n) for n in (
             "s_ready", "mx_ready", "s_sub", "p_ready", "gv_done", "gvbd_ready", "v_done", "vrows_ready", "v_stored",
             "vbd_loaded", "masks_loaded",
             "ls_ready", "lmx_ready", "ls_sub", "pl_ready", "gates_done", "tg_ready"))
        (pt_done, pt_copied, lpt_done, lpt_copied, pv_done, rden_ready, a_ready, ag_ready, lpv_done, rlden_ready,
         remn_ready, rem_done, remg_ready, att_ready, y_done, yga_ready, x1_ready) = (sem(n) for n in (
             "pt_done", "pt_copied", "lpt_done", "lpt_copied", "pv_done", "rden_ready", "a_ready", "ag_ready",
             "lpv_done", "rlden_ready", "remn_ready", "rem_done", "remg_ready", "att_ready", "y_done",
             "yga_ready", "x1_ready"))
        (stat_d, aggr_d, eps_d, rstd_d_s, xn_d_s, x2T_done, h2T_ready, hid_done, hid_summed) = (
            sem(n) for n in ("stat_d", "aggr_d", "eps_d", "rstd_d_s", "xn_d_s", "x2T_done", "h2T_ready",
                             "hid_done", "hid_summed"))
        (g_done, g_ready, mix_done, mixed, ffn1_done, gelu_done, ffn2_done, fT_ready, fin_done, o_ready) = (
            sem(n) for n in ("g_done", "g_ready", "mix_done", "mixed", "ffn1_done", "gelu_done", "ffn2_done",
                             "fT_ready", "fin_done", "o_ready"))
        stored = [sem(f"stored{k}") for k in range(2)]

        def bc(ap, shape, *axes):
            for a in axes:
                ap = ap.unsqueeze(a)
            return ap.to_broadcast(shape)

        def at_least(eng, s, value):
            if not isinstance(value, int) or value > 0:
                eng.wait_ge(s, value)

        def bank_free(eng, it, *users):
            for lag, s, per, n in users:
                b = it - lag
                if isinstance(it, int) and not 0 <= b < B:
                    continue
                at_least(eng, s, per * b + n)
                return

        def pipeline(eng, step, after=None):
            for it in range(4):
                step(it)
                if after is not None:
                    after(it)
            with eng.Fori(4, B) as it:
                step(it)
            for it in range(B, B + 4):
                step(it)
                if after is not None:
                    after(it)

        def has(it, lag):
            return not isinstance(it, int) or 0 <= it - lag < B


        ga_dram = nc.dram_tensor("ga_rows", (B, D), F32, kind="Internal").ap()
        v_dram = nc.dram_tensor("v_rows", (S, 4, HD * G), F32, kind="Internal").ap()
        block = ctx.enter_context(nc.Block())

        def column(a):
            return a.rearrange("(p a) -> p a", a=1)

        mod_w = [(c_rows, ins["L0_c"]), (wmod, ins["L0_wmod"])]
        attn_w = [
            (wk, ins["L0_attn_wk"]), (wq, ins["L0_attn_wq"]), (wgq, ins["L0_attn_wgq"]), (wgk, ins["L0_attn_wgk"]),
            (gate_col[:, 0:1], ins["L0_attn_gate_local_w"].rearrange("h (d a) -> (h d) a", a=1)),
            (gate_col[:, 1:2], ins["L0_attn_gate_remote_w"].rearrange("h (d a) -> (h d) a", a=1)),
            (wv_in, ins["L0_attn_wv"]), (wgv, ins["L0_attn_wgv"]), (w_out, ins["L0_attn_w_out"]),
        ]
        rest_w = [
            (W1, ins["L0_ffn_W1"].rearrange("(c p) h -> p c h", p=P)), (W2, ins["L0_ffn_W2"]),
            (gate_w1, ins["L0_ffn_gate_w1"]), (gate_w2, ins["L0_ffn_gate_w2"]),
            (gate_b1, column(ins["L0_ffn_gate_b1"])), (gate_b2, column(ins["L0_ffn_gate_b2"])),
            (b2_col, column(ins["L0_ffn_b2"])), (tb1, ins["L0_ffn_Tb1"]), (tb2, ins["L0_ffn_Tb2"]),
        ] + [(b1_col[:, c:c + 1], column(ins["L0_ffn_b1"][c * P:(c + 1) * P])) for c in range(FC)] + [
            (r_out[0:NL, 0, :], ins["L0_attn_r_out_w"]), (r_out[NL:P, 1, :], ins["L0_attn_r_out_w"]),
        ]
        N_G0 = 1 + 1 + FC + 1
        N_G = N_G0 + 1 + (NG - 1) + FC + 1
        N_MOD, N_ATTN, N_W, N_TW = 16 * len(mod_w), 16 * len(attn_w), 16 * len(rest_w), 16 * 2 * E

        @block.sync
        def _(sp):
            def load_x(b):
                sp.dma_start(x_all[:, bass.ds(b * S, S)].rearrange("p (t d) -> p t d", t=T),
                             x_d[bass.ds(b, 1)].rearrange("b (t p) d -> p (b t) d", p=P)).then_inc(x_loaded, 16)

            def load(weights, loaded):
                for dst, src in weights:
                    sp.dma_start(dst[:] if not isinstance(dst, bass.AP) else dst, src).then_inc(loaded, 16)

            load_x(0)
            load(mod_w, mod_loaded)
            load(attn_w, attn_loaded)

            def step(it):
                if has(it, 0):
                    sp.wait_ge(x_loaded, 16 * (it + 1))
                    if not isinstance(it, int) or it + 1 < B:
                        load_x(it + 1)
                if has(it, 1):
                    sp.wait_ge(vrows_ready, it)
                    sp.dma_start(v_dram.rearrange("(t p) h n -> p t (h n)", p=P), V_rows[:]).then_inc(v_stored, 16)
                    sp.wait_ge(km_ready, it)
                    for g in range(G):
                        sp.dma_start(KBD[W * g:W * g + W, 4 * g:4 * g + 4, W:KW], KM[W * g:W * g + W]
                                     ).then_inc(kbd_loaded, 16)
                    sp.wait_ge(v_stored, 16 * it)
                    sp.wait_ge(pv_done, it)
                    for h in range(4):
                        sp.dma_start(VBD[W * h:W * h + W, :, h, :], v_dram[:, h, :].rearrange("(k c) n -> c k n", c=W)
                                     ).then_inc(vbd_loaded, 16)

            step(0)
            sp.wait_ge(zeros_ready, 1)
            load(rest_w, w_loaded)
            sp.wait_ge(zeros_ready, 2)
            sp.wait_ge(masks_ready, 1)
            for q in range(4):
                heads = slice(8, 16) if q < 2 else slice(0, 8)
                sp.dma_start(KBD[W * q:W * q + W, heads, :], bc(mask_rows[W * q:W * q + W, :], [W, 8, KW], 1)
                             ).then_inc(masks_loaded, 16)
            step(1)
            step(2)
            with sp.Fori(3, B - 1) as it:
                step(it)
            step(B - 1)
            step(B)

            with sp.Fori(0, NG) as g:
                for j in range(GB):
                    sp.wait_ge(o_ready, g * GB + (j + 1))
                    sp.dma_start(out[bass.ds(g * GB + j, 1)].rearrange("b (t p) d -> p (b t) d", p=P),
                                 o_sb[j % 2][:].rearrange("p (t d) -> p t d", t=T)).then_inc(stored[j % 2], 16)
            for k in range(2):
                sp.wait_ge(stored[k], 16 * B // 2)

        @block.gpsimd
        def _(pool):
            nc.gpsimd.memset(ident[:], 0.0).then_inc(mask_ready, 1)
            pool.wait_ge(mask_ready, 1)
            nc.gpsimd.affine_select(out=ident[:], in_=ident[:], compare_op=ALU.not_equal, fill=1.0, base=0,
                                    pattern=[[-1, P]], channel_multiplier=1).then_inc(mask_ready, 1)
            nc.gpsimd.memset(minus_half[:], -0.5).then_inc(mask_ready, 1)
            nc.gpsimd.memset(eps_row[:], 1e-5).then_inc(mask_ready, 1)
            nc.gpsimd.memset(r_out[:], 0.0).then_inc(zeros_ready, 1)
            nc.gpsimd.memset(tri[:], 1.0).then_inc(mask_ready, 1)
            nc.gpsimd.memset(KBD[:], 0.0).then_inc(zeros_ready, 1)
            pool.wait_ge(mask_ready, 5)
            nc.gpsimd.affine_select(out=tri[:], in_=tri[:], compare_op=ALU.is_ge, fill=0.0, base=0,
                                    pattern=[[-1, P]], channel_multiplier=1).then_inc(mask_ready, 1)
            nc.gpsimd.memset(VBD[:], 0.0).then_inc(pv_done, 1)

            def load_experts(e):
                pool.dma_start(TW1[J * e:J * e + J], ins["L0_ffn_TW1"][e].rearrange("(i j) h -> j i h", j=J)
                               ).then_inc(tw_loaded, 16)
                pool.dma_start(TW2[J * e:J * e + J], ins["L0_ffn_TW2"][e].rearrange("(i j) f -> j i f", j=J)
                               ).then_inc(tw_loaded, 16)

            def inv_std(b, aggr, mv, ve, eps, rstd, rstd_s):
                pool.wait_ge(aggr, T * (b + 1))
                nc.gpsimd.tensor_tensor(ve[:], mv[:, :, 1], eps_row[:], ALU.add).then_inc(eps, 1)
                pool.wait_ge(eps, b + 1)
                nc.gpsimd.tensor_tensor(rstd[:], ve[:], minus_half[:], ALU.pow).then_inc(rstd_s, 1)

            def step(it):
                if has(it, 1):
                    b = it - 1
                    pool.wait_ge(k_ready, b + 1)
                    nc.gpsimd.tensor_tensor(KM[:], bc(K_ch[:], [P, 4, S], 1), bc(bd_scale[:], [P, 4, S], 2), ALU.mult
                                            ).then_inc(km_ready, 1)
                if has(it, 0):
                    inv_std(it, aggr_a, mv_a, ve_a, eps_a, rstd_a, rstd_a_s)
                if has(it, 4):
                    inv_std(it - 4, aggr_d, mv_d, ve_d, eps_d, rstd_d, rstd_d_s)
                if has(it, 2):
                    b = it - 2
                    both = PT[:, 0:G * 2 * S].rearrange("p (g k s) -> p g k s", g=G, k=2)
                    for t in range(T):
                        pool.wait_ge(pt_copied, 4 * b + 2 * (t + 1))
                        tile = slice(t * P, (t + 1) * P)
                        nc.gpsimd.tensor_tensor(PT_sum[:, :, tile], both[:, :, 0, tile], both[:, :, 1, tile], ALU.add
                                                ).then_inc(pts_ready, 1)
                if has(it, 1):
                    b = it - 1
                    pool.wait_ge(gq_ready, 2 * (b + 1))
                    nc.gpsimd.tensor_tensor(GKBD[0:NL], bc(GKT[:], [NL, LH, NL], 1),
                                            bc(head[0:NL, 0:LH], [NL, LH, NL], 2), ALU.mult).then_inc(gkbd_ready, 1)
                if has(it, 3):
                    b = it - 3
                    pool.wait_ge(yga_ready, b + 1)
                    xb = x_all[:, bass.ds(b * S, S)]
                    nc.gpsimd.tensor_tensor(xb, xb, y_ga[:], ALU.add).then_inc(x1_ready, 1)
                if has(it, 2):
                    b = it - 2
                    pool.wait_ge(ag_ready, b + 1)
                    pool.wait_ge(remg_ready, b + 1)
                    at_least(pool, y_done, b)
                    nc.gpsimd.tensor_tensor(attT[:], a_gated[:], rem_g[:], ALU.add).then_inc(att_ready, 1)

            def after(it):
                if it == 0:
                    pool.wait_ge(head_ready, 1)
                if it == 1:
                    pool.wait_ge(ga_ready, 1)
                    pool.dma_start(ga_dram, ga_row).then_inc(ga_stored, 16)
                    pool.wait_ge(ga_stored, 16)
                    pool.dma_start(GA[:], bc(ga_dram.rearrange("b d -> (b d)"), [P, B * D], 0)).then_inc(ga_loaded, 16)
                if 1 <= it < 4 or it == B:
                    for e in range(2 * (it - 1), 2 * it) if it < 4 else range(6, E):
                        load_experts(e)

            pipeline(pool, step, after)

        @block.scalar
        def _(act):
            act.wait_ge(mod_loaded, N_MOD)
            nc.scalar.activation(silu_a[:], c_rows[:], ACT.Exp, scale=-1.0).then_inc(silu_exp, 1)
            act.wait_ge(siluT_done, 1)
            nc.scalar.copy(siluT[:], WB[1][:, 0:B]).then_inc(siluT_ready, 1)

            def probs(b, k):
                act.wait_ge(s_sub, 4 * b + (k + 1))
                nc.scalar.activation(Pr[:, k, :], Pr[:, k, :], ACT.Exp).then_inc(p_ready, 1)

            def step(it):
                if has(it, 1):
                    b = it - 1
                    act.wait_ge(qk_done, b + 1)
                    at_least(act, km_ready, b)
                    nc.scalar.copy(K_ch[:], WB[0][:, S:2 * S]).then_inc(k_ready, 1)
                    for k in range(2):
                        nc.scalar.copy(QT[k][64 * k:64 * k + 64, :], WB[0][64 * k:64 * k + 64, 0:S]).then_inc(qt_ready, 1)
                if has(it, 2):
                    probs(it - 2, 1)
                if has(it, 1):
                    act.wait_ge(gqk_done, b + 1)
                    nc.scalar.activation(GQT[0:NL], WB[1][0:NL, 0:S], ACT.Copy, scale=SCALE / POOL).then_inc(gq_ready, 1)
                    nc.scalar.copy(GKT[:], WB[1][0:NL, S:S + NL]).then_inc(gq_ready, 1)
                if has(it, 2):
                    probs(it - 2, 2)
                if has(it, 1):
                    b = it - 1
                    act.wait_ge(v_done, b + 1)
                    at_least(act, vbd_loaded, N_VBD * b)
                    nc.scalar.copy(V_rows[:].rearrange("p t n -> p (t n)"), WB[3][:, 0:T * D]).then_inc(vrows_ready, 1)
                if has(it, 2):
                    probs(it - 2, 3)
                if has(it, 2):
                    b = it - 2
                    if isinstance(it, int) and it == 2:
                        act.wait_ge(ga_stored, 16)
                    act.wait_ge(lpt_done, 2 * b + 1)
                    nc.scalar.copy(PL[:, :, 0:S].rearrange("p g (t s) -> p t g s", t=T),
                                   WB[0][:].rearrange("p (t g s) -> p t g s", t=T, g=LG)).then_inc(lpt_copied, 1)
                    act.wait_ge(lpt_done, 2 * b + 2)
                    nc.scalar.copy(PL[:, :, S:S + P],
                                   WB[1][:, 0:2 * P].rearrange("p (g s) -> p g s", g=LG)).then_inc(lpt_copied, 1)
                    for q in range(4):
                        act.wait_ge(pt_done, 4 * b + (q + 1))
                        t, gp = divmod(q, 2)
                        dst = PT[:, gp * 4 * S:(gp + 1) * 4 * S].rearrange("p (k s) -> p k s", s=S)[:, :, t * P:(t + 1) * P]
                        nc.scalar.copy(dst, SB[q][:].rearrange("p (k s) -> p k s", s=P)).then_inc(pt_copied, 1)
                if has(it, 4):
                    b = it - 4
                    act.wait_ge(x2T_done, b + 1)
                    nc.scalar.activation(h2T[:, bass.ds(b * S, S)], SB[0][:, 0:S], ACT.Identity,
                                         scale=cb1T[:, bass.ds(b, 1)], bias=sbT[:, bass.ds(b, 1)]).then_inc(h2T_ready, 1)
                    act.wait_ge(hid_done, b + 1)
                    nc.scalar.activation(SB[1][:, 0:S], SB[1][:, 0:S], ACT.Relu, bias=gate_b1[:],
                                         accum_out=hsum[:, bass.ds(b, 1)]).then_inc(hid_summed, 1)
                if has(it, 0):
                    act.wait_ge(xT_done, it + 1)
                    at_least(act, hp_ready, it)
                    if isinstance(it, int) and it == 0:
                        act.wait_ge(mod_ready, 4)
                    nc.scalar.activation(hT[:], SB[0][:, 0:S], ACT.Identity, scale=ca1T[:, bass.ds(it, 1)],
                                         bias=saT[:, bass.ds(it, 1)]).then_inc(hT_ready, 1)
                if has(it, 1):
                    b = it - 1
                    for t, pl in ((0, PlA), (1, PlB)):
                        act.wait_ge(ls_sub, 2 * b + (t + 1))
                        nc.scalar.activation(pl[:], pl[:], ACT.Exp).then_inc(pl_ready, 1)
                    act.wait_ge(gates_done, b + 1)
                    at_least(act, ag_ready, b)
                    at_least(act, remg_ready, b)
                    nc.scalar.activation(tg[:].rearrange("p k s -> p (k s)"), WB[2][:], ACT.Tanh, scale=0.5
                                         ).then_inc(tg_ready, 1)
                    probs(b, 0)

            def after(it):
                if it == 0:
                    act.wait_ge(wqT_done, 1)
                    nc.scalar.copy(wqT, SB[1][:, 0:D]).then_inc(wqT_ready, 1)
                    act.wait_ge(gate_w_done, 1)
                    for k in range(2):
                        nc.scalar.copy(gate_w[:, k, :].rearrange("p (h d) -> p h d", d=HD),
                                       bc(SB[2][:, k * H:(k + 1) * H], [P, H, HD], 2)).then_inc(gate_w_ready, 1)
                if it == 1:
                    act.wait_ge(wT_done, 1)
                    nc.scalar.copy(W1T[:], WB[3][:]).then_inc(wT_ready, 1)
                    act.wait_ge(wT_done, 2)
                    nc.scalar.copy(W2T[:].rearrange("p c h -> p (c h)"), WB[3][:]).then_inc(wT_ready, 1)
                    act.wait_ge(wT_done, 3)
                    nc.scalar.copy(gate_w1T[:], WB[3][:, 0:P]).then_inc(wT_ready, 1)
                    nc.scalar.copy(gate_w2T[:], WB[3][:, P:P + E]).then_inc(wT_ready, 1)

            pipeline(act, step, after)

            with act.Fori(0, NG) as g:
                for j in range(GB):
                    act.wait_ge(ffn1_done, g * GB + (j + 1))
                    if j >= 2:
                        act.wait_ge(ffn2_done, g * GB + (j - 1))
                    for c in range(FC):
                        nc.scalar.activation(u[j % 2][:, c, :], WB[2 * (j % 2) + c // 2][:, (c % 2) * S:(c % 2 + 1) * S],
                                             ACT.Gelu_apprx_tanh, bias=mb1T[:, c, bass.ds(g * GB + j, 1)]
                                             ).then_inc(gelu_done, 1)

        @block.vector
        def _(dve):
            n = [0]
            chain = sem("setup_chain")

            def beside(ins_):
                n[0] += 1
                ins_.then_inc(chain, 1)

            def then(ins_):
                beside(ins_)
                dve.wait_ge(chain, n[0])

            dve.wait_ge(silu_exp, 1)
            then(nc.vector.tensor_scalar(silu_b[:], silu_a[:], 1.0, None, ALU.add))
            then(nc.vector.reciprocal(silu_c[:], silu_b[:]))
            nc.vector.tensor_tensor(silu_b[:], silu_c[:], c_rows[:], ALU.mult).then_inc(silu_ready, 1)
            dve.wait_ge(mask_ready, 2)
            beside(nc.vector.tensor_reduce(quad[:], ident[:].rearrange("p (h c) -> p h c", h=4), AX.X, ALU.add))
            then(nc.vector.tensor_reduce(head[:], ident[:].rearrange("p (h d) -> p h d", d=HD), AX.X, ALU.add))
            then(nc.vector.tensor_reduce(bd_scale[:], head[:].rearrange("p (g h) -> p h g", h=4), AX.X, ALU.add))
            then(nc.vector.tensor_scalar(bd_scale[:], bd_scale[:], SCALE, None, ALU.mult))
            nc.vector.memset(wait_carrier[:], 0.0).then_inc(head_ready, 1)
            def modulation():
                dve.wait_ge(mod_done, 1)
                for dst, k, add in ((saT, 0, 0.0), (ca1T, 1, 1.0), (sbT, 2, 0.0), (cb1T, 3, 1.0)):
                    nc.vector.tensor_scalar(dst[:], WB[0][:, k * B:(k + 1) * B], add, None, ALU.add).then_inc(mod_ready, 1)

            def stats(src, st, stat, mv, aggr, b):
                for t in range(T):
                    nc.vector.bn_stats(st[:, t, :], src[:, t * D:(t + 1) * D]).then_inc(stat, 1)
                dve.wait_ge(stat, T * (b + 1))
                nc.vector.memset(wait_carrier[:], 0.0)
                for t in range(T):
                    nc.vector.bn_aggr(mv[:, t, :], st[:, t, :]).then_inc(aggr, 1)

            def normed(src, mv, rstd, xn, xn_s):
                for t in range(T):
                    nc.vector.tensor_scalar(xn[:, t, :], src[:, t * D:(t + 1) * D], mv[:, t, 0:1], rstd[:, t:t + 1],
                                            ALU.subtract, ALU.mult).then_inc(xn_s, 1)

            def maximum(b, k):
                dve.wait_ge(s_ready, 4 * b + (k + 1))
                nc.vector.tensor_reduce(mx[:, k, :], SB[k][:].rearrange("p (h j) -> p h j", h=8), AX.X, ALU.max
                                        ).then_inc(mx_ready, 1)

            def lowered(b, k):
                dve.wait_ge(mx_ready, 4 * b + (k + 1))
                at_least(dve, pt_done, 4 * b + (k - 3))
                nc.vector.tensor_tensor(Pr[:, k, :].rearrange("p (w h c) -> p h w c", w=2, h=8),
                                        SB[k][:].rearrange("p (h w c) -> p h w c", w=2, h=8),
                                        bc(mx[:, k, :], [P, 8, 2, W], 2, 2), ALU.subtract).then_inc(s_sub, 1)

            latent_tiles = ((0, PlA, W), (1, PlB, NL))

            def latent_maximum(b, t, m):
                dve.wait_ge(ls_ready, 2 * b + (t + 1))
                nc.vector.tensor_reduce(lmx[:, t, :], WB[1 - t][:, 0:LH * m].rearrange("p (h j) -> p h j", h=LH),
                                        AX.X, ALU.max).then_inc(lmx_ready, 1)

            def latent_lowered(b, t, pl, m):
                dve.wait_ge(lmx_ready, 2 * b + (t + 1))
                at_least(dve, lpt_done, 2 * b)
                nc.vector.tensor_tensor(pl[:].rearrange("p k (h n) -> p h k n", n=W),
                                        WB[1 - t][:, 0:LH * m].rearrange("p (h k n) -> p h k n", h=LH, n=W),
                                        bc(lmx[:, t, :], [P, LH, m // W, W], 2, 2), ALU.subtract).then_inc(ls_sub, 1)

            def output_times_ga(b):
                dve.wait_ge(y_done, b + 1)
                if isinstance(b, int) and b == 0:
                    dve.wait_ge(ga_loaded, 16)
                at_least(dve, x1_ready, b)
                nc.vector.tensor_tensor(y_ga[:].rearrange("p (t d) -> p t d", t=T),
                                        WB[3][:, 0:S].rearrange("p (t d) -> p t d", t=T),
                                        bc(GA[:, bass.ds(b * D, D)], [P, T, D], 1), ALU.mult).then_inc(yga_ready, 1)

            def step(it):
                tail = isinstance(it, int) and it >= B + 2
                if tail and has(it, 3):
                    output_times_ga(it - 3)
                if has(it, 0):
                    dve.wait_ge(x_loaded, 16 * (it + 1))
                    stats(x_all[:, bass.ds(it * S, S)], st_a, stat_a, mv_a, aggr_a, it)
                if has(it, 4):
                    dve.wait_ge(x1_ready, it - 4 + 1)
                    stats(x_all[:, bass.ds((it - 4) * S, S)], st_d, stat_d, mv_d, aggr_d, it - 4)
                if has(it, 0):
                    dve.wait_ge(rstd_a_s, it + 1)
                    at_least(dve, xT_done, it)
                    normed(x_all[:, bass.ds(it * S, S)], mv_a, rstd_a, xn_a, xn_a_s)
                    if isinstance(it, int) and it == 0:
                        modulation()
                if has(it, 4):
                    b = it - 4
                    dve.wait_ge(rstd_d_s, b + 1)
                    at_least(dve, x2T_done, b)
                    normed(x_all[:, bass.ds(b * S, S)], mv_d, rstd_d, xn_d, xn_d_s)
                if has(it, 2):
                    b = it - 2
                    dve.wait_ge(lpv_done, b + 1)
                    nc.vector.reciprocal(rlden[:], WB[0][:, P:2 * P]).then_inc(rlden_ready, 1)
                    dve.wait_ge(rlden_ready, b + 1)
                    at_least(dve, rem_done, b)
                    nc.vector.tensor_tensor(rem_n[:], WB[0][:, 0:P], rlden[:], ALU.mult).then_inc(remn_ready, 1)
                if has(it, 1):
                    b = it - 1
                    dve.wait_ge(gv_done, b + 1)
                    at_least(dve, lpv_done, b)
                    nc.vector.tensor_tensor(GVBD[:].rearrange("p k g (h d) -> p (k g) h d", h=4),
                                            bc(WB[1][:, 0:2 * LG * HD].rearrange("p (n d) -> p n d", d=HD), [P, 2 * LG, 4, HD], 2),
                                            bc(pool_bd[:].rearrange("p (h d) -> p h d", h=4), [P, 2 * LG, 4, HD], 1),
                                            ALU.mult).then_inc(gvbd_ready, 1)
                if has(it, 3) and not tail:
                    output_times_ga(it - 3)
                if has(it, 2):
                    b = it - 2
                    dve.wait_ge(pv_done, b + 2)
                    nc.vector.reciprocal(rden[:], SB[2][:, S:2 * S]).then_inc(rden_ready, 1)
                    dve.wait_ge(rden_ready, b + 1)
                    nc.vector.tensor_tensor(a_loc[:], SB[2][:, 0:S], rden[:], ALU.mult).then_inc(a_ready, 1)
                if has(it, 0):
                    dve.wait_ge(hT_ready, it + 1)
                    nc.vector.tensor_reduce(hpT[:], hT[:].rearrange("p (n k) -> p n k", k=POOL), AX.X, ALU.add
                                            ).then_inc(hp_ready, 1)
                if has(it, 2):
                    b = it - 2
                    dve.wait_ge(a_ready, b + 1)
                    dve.wait_ge(tg_ready, b + 1)
                    at_least(dve, att_ready, b)
                    nc.vector.scalar_tensor_tensor(a_gated[:], tg[:, 0, :], 1.0, a_loc[:], ALU.add, ALU.mult).then_inc(ag_ready, 1)
                    dve.wait_ge(rem_done, b + 1)
                    nc.vector.scalar_tensor_tensor(rem_g[:], tg[:, 1, :], 1.0, WB[3][:, 0:S], ALU.add, ALU.mult
                                                   ).then_inc(remg_ready, 1)
                if has(it, 1):
                    b = it - 1
                    for t, pl, m in latent_tiles:
                        latent_maximum(b, t, m)
                    latent_lowered(b, *latent_tiles[0])
                    maximum(b, 0)
                    latent_lowered(b, *latent_tiles[1])
                    for k in range(4):
                        if k < 3:
                            maximum(b, k + 1)
                        lowered(b, k)

            def mixed_rows(g, m):
                dve.wait_ge(mix_done, g * 16 + (m + 1))
                psum = (WB if m < 8 else SB)[m % 4][:].rearrange("p (r b) -> p r b", b=GB)
                if m < 8:
                    dst = mW1[:, :, m * 64:(m + 1) * 64].rearrange("p b r -> p r b")
                    base = W1T[:, m * 64:(m + 1) * 64]
                else:
                    c, half = divmod(m - 8, 2)
                    dst = mW2[:, c, :, half * 64:half * 64 + 64].rearrange("p b r -> p r b")
                    base = W2T[:, c, half * 64:half * 64 + 64]
                nc.vector.tensor_tensor(dst, psum, bc(base, [P, 64, GB], 2), ALU.add).then_inc(mixed, 1)

            def experts(g0, g1, done):
                cols = slice(g0 * GB, g1 * GB)
                n_b = (g1 - g0) * GB
                dve.wait_ge(g_done, done + 1)
                nc.vector.tensor_scalar(gT[:, cols], WB[2][0:E, 0:n_b] if g0 == 0 else SB[0][0:E, 0:n_b], 1.0 / S,
                                        gate_b2[:], ALU.mult, ALU.add).then_inc(g_ready, 1)
                dve.wait_ge(g_done, done + 2)
                rows, biases = (WB[2], SB[3]) if g0 == 0 else (SB[1], SB[2])
                for g in range(g0, g1):
                    nc.vector.tensor_tensor(Gd[:, g * J * GB:(g + 1) * J * GB].rearrange("p (j b) -> p j b", j=J),
                                            bc(rows[:, (g - g0) * GB:(g - g0 + 1) * GB], [P, J, GB], 1),
                                            bc(jmask[:], [P, J, GB], 2), ALU.mult).then_inc(g_ready, 1)
                dve.wait_ge(g_done, done + 3)
                for c in range(FC):
                    nc.vector.tensor_scalar(mb1T[:, c, cols], biases[:, c * n_b:(c + 1) * n_b], b1_col[:, c:c + 1], None,
                                            ALU.add).then_inc(g_ready, 1)
                then(nc.vector.tensor_scalar(mb2T[:, cols], biases[:, FC * n_b:(FC + 1) * n_b], b2_col[:], None, ALU.add))
                nc.vector.tensor_tensor(gmb2T[:, cols], mb2T[:, cols], gbT[:, cols], ALU.mult).then_inc(g_ready, 1)

            def after(it):
                if it == B + 1:
                    experts(0, 1, 0)
                if it == B + 3:
                    for m in range(8):
                        mixed_rows(0, m)
                    experts(1, NG, 3)
                if it == 0:
                    dve.wait_ge(attn_loaded, N_ATTN)
                    beside(nc.vector.tensor_copy(wv[:].rearrange("p (h d g) -> p g h d", h=4, d=HD),
                                               wv_in[:].rearrange("p (g h d) -> p g h d", g=G, h=4)))
                    then(nc.vector.tensor_tensor(gate_cols[:, 0:2 * H].rearrange("p (k h) -> p k h", k=2), bc(head[:], [P, 2, H], 1),
                                                 bc(gate_col[:], [P, 2, H], 2), ALU.mult))
                    nc.vector.tensor_scalar(w_out_half[:], w_out[:], 0.5, None, ALU.mult).then_inc(attn_w_ready, 1)
                    for g, sign, size, dst in ((WB[2][0:B, 0:D], ga_sign, ga_abs, ga_row), (WB[2][:, P:P + B], gb_sign, gb_abs, gbT)):
                        then(nc.vector.tensor_scalar(sign[:], g, 0.0, 2.0, ALU.is_ge, ALU.mult))
                        then(nc.vector.scalar_tensor_tensor(size[:], sign[:], -1.0, g, ALU.add, ALU.mult))
                        then(nc.vector.tensor_scalar(size[:], size[:], 0.25, None, ALU.max))
                        then(nc.vector.scalar_tensor_tensor(dst[:], sign[:], -1.0, size[:], ALU.add, ALU.mult))
                    nc.vector.memset(wait_carrier[:], 0.0).then_inc(ga_ready, 1)
                    dve.wait_ge(mask_ready, 6)
                    then(nc.vector.tensor_copy(ones_bd[:].rearrange("p (h d) -> p h d", h=4), bc(quad[:], [P, 4, HD], 2)))
                    then(nc.vector.tensor_scalar(pool_bd[:], ones_bd[:], 1.0 / POOL, None, ALU.mult))
                    then(nc.vector.tensor_tensor(tri4[:].rearrange("p (k c) -> p k c", k=4), tri[:].rearrange("p (k c) -> p k c", k=4),
                                                 bc(quad[:], [P, 4, W], 2), ALU.mult))
                    then(nc.vector.tensor_reduce(cur[:], tri4[:].rearrange("p (k c) -> p c k", k=4), AX.X, ALU.add))
                    beside(nc.vector.tensor_scalar(win[:, 0:W], cur[:], -BIG, None, ALU.mult))
                    then(nc.vector.tensor_scalar(win[:, W:HALF], cur[:], 1.0, BIG, ALU.subtract, ALU.mult))
                    for q in range(4):
                        rows = slice(W * q, W * q + W)
                        first = 0 if q % 2 == 0 else W
                        beside(nc.vector.tensor_copy(mask_rows[rows, first:first + S].rearrange("p (k j) -> p k j", j=HALF),
                                                   bc(win[rows, :], [W, S // HALF, HALF], 1)))
                        if q % 2 == 0:
                            then(nc.vector.tensor_copy(mask_rows[rows, S:KW], win[rows, 0:W]))
                            then(nc.vector.memset(mask_rows[rows, 0:W], -BIG))
                        else:
                            beside(nc.vector.tensor_copy(mask_rows[rows, 0:W], win[rows, W:HALF]))
                    for k, half in ((0, slice(64, P)), (1, slice(0, 64))):
                        beside(nc.vector.tensor_copy(QT[k][half, :].rearrange("p (n j) -> p n j", j=64), bc(ident[half, half], [64, S // 64, 64], 1)))
                    beside(nc.vector.tensor_copy(GQT[NL:P, :].rearrange("p (n k) -> p n k", k=POOL), bc(ident[NL:P, NL:P], [NL, NL, POOL], 2)))
                    beside(nc.vector.tensor_scalar(GKBD[NL:P], bc(tri[NL:P, NL:P], [NL, LH, NL], 1), 1.0, BIG, ALU.subtract, ALU.mult))
                    beside(nc.vector.tensor_copy(e_rows[:], bc(ident[0:E, 0:E], [E, E, J], 2)))
                    then(nc.vector.tensor_reduce(jmask[:], ident[:].rearrange("p (e j) -> p j e", j=J), AX.X, ALU.add))
                    nc.vector.memset(wait_carrier[:], 0.0).then_inc(masks_ready, 1)

            pipeline(dve, step, after)

            def out_row(g, j):
                dve.wait_ge(fin_done, g * GB + (j + 1))
                if j >= 2:
                    dve.wait_ge(stored[j % 2], g * (16 * GB // 2) + 16 * (j // 2))
                nc.vector.tensor_tensor(o_sb[j % 2][:], SB[2 + j % 2][:, 0:S], x_all[:, bass.ds((g * GB + j) * S, S)],
                                        ALU.add).then_inc(o_ready, 1)

            def group(g, last):
                for m in range(8, 16):
                    mixed_rows(g, m)
                for j in range(GB):
                    dve.wait_ge(ffn2_done, g * GB + (j + 1))
                    if j >= 2:
                        dve.wait_ge(fin_done, g * GB + (j - 1))
                    nc.vector.tensor_scalar(fT[j % 2][:], SB[j % 2][:, 0:S], gbT[:, bass.ds(g * GB + j, 1)],
                                            gmb2T[:, bass.ds(g * GB + j, 1)], ALU.mult, ALU.add).then_inc(fT_ready, 1)
                    if not last and j >= GB - 2:
                        for m in range(4 * (j - GB + 2), 4 * (j - GB + 3)):
                            mixed_rows(g + 1, m)
                    if j >= 1:
                        out_row(g, j - 1)
                out_row(g, GB - 1)
                for k in range(2):
                    dve.wait_ge(stored[k], (g + 1) * (16 * GB // 2))

            dve.wait_ge(g_ready, N_G)
            with dve.Fori(0, NG - 1) as g:
                group(g, False)
            group(NG - 1, True)

        @block.tensor
        def _(pe):
            mm = nc.tensor.matmul
            pe.wait_ge(mask_ready, 2)
            pe.wait_ge(silu_ready, 1)
            nc.tensor.transpose(WB[1][:, 0:B], silu_b[:], ident[0:B, 0:B]).then_inc(siluT_done, 1)
            pe.wait_ge(siluT_ready, 1)
            for n, k in enumerate((0, 1, 3, 4)):
                mm(WB[0][:, n * B:(n + 1) * B], wmod[:, k * D:(k + 1) * D], siluT[:], start=True, stop=True)
            mm(WB[2][:, P:P + B], wmod[:, 5 * D:6 * D], siluT[:], start=True, stop=True)
            mm(WB[2][0:B, 0:D], siluT[:], wmod[:, 2 * D:3 * D], start=True, stop=True).then_inc(mod_done, 1)

            def mix(g, m):
                for k in range(4):
                    if m < 8:
                        lhsT = TW1[:, 4 * m + k, :]
                    else:
                        c, half = divmod(m - 8, 2)
                        lhsT = TW2[:, 4 * half + k, c * P:(c + 1) * P]
                    last = mm((WB if m < 8 else SB)[m % 4][:, k * P:(k + 1) * P], lhsT,
                              Gd[:, bass.ds(g * (J * GB), J * GB)], start=True, stop=True)
                last.then_inc(mix_done, 1)

            def ffn1(g, j):
                if j == 1:
                    pe.wait_ge(mixed, g * 16 + 8)
                if j >= 2:
                    pe.wait_ge(gelu_done, g * (FC * GB) + FC * (j - 1))
                for c in range(FC):
                    if j == 0:
                        pe.wait_ge(mixed, g * 16 + max(2 * (c + 1), 5 + c // 2))
                    last = mm(WB[2 * (j % 2) + c // 2][:, (c % 2) * S:(c % 2 + 1) * S], mW1[:, j, c * P:(c + 1) * P],
                              h2T[:, bass.ds((g * GB + j) * S, S)], start=True, stop=True)
                last.then_inc(ffn1_done, 1)

            def ffn2(g, j):
                pe.wait_ge(gelu_done, g * (FC * GB) + FC * (j + 1))
                if j >= 2:
                    pe.wait_ge(fT_ready, g * GB + (j - 1))
                for c in range(FC):
                    if j == 0:
                        pe.wait_ge(mixed, g * 16 + 8 + max(2 * (c + 1), 5))
                    last = mm(SB[j % 2][:, 0:S], mW2[:, c, j, :], u[j % 2][:, c, :], start=(c == 0), stop=(c == FC - 1))
                last.then_inc(ffn2_done, 1)

            def final_T(g, j):
                pe.wait_ge(fT_ready, g * GB + (j + 1))
                if j >= 2:
                    pe.wait_ge(o_ready, g * GB + (j - 1))
                for t in range(T):
                    last = nc.tensor.transpose(SB[2 + j % 2][:, t * P:(t + 1) * P], fT[j % 2][:, t * P:(t + 1) * P], ident[:])
                last.then_inc(fin_done, 1)

            def projections(it):
                b = it - 1
                pe.wait_ge(hT_ready, b + 1)
                bank_free(pe, it, (2, ls_sub, 2, 2))
                mm(WB[0][:, S:2 * S], wk[:], hT[:], start=True, stop=True)
                mm(WB[0][:, 0:S], wq[:], hT[:], start=True, stop=True).then_inc(qk_done, 1)
                pe.wait_ge(hp_ready, b + 1)
                bank_free(pe, it, (2, ls_sub, 2, 1))
                mm(WB[1][0:NL, 0:S], wgq[:], hT[:], start=True, stop=True)
                mm(WB[1][0:NL, S:S + NL], wgk[:], hpT[:], start=True, stop=True).then_inc(gqk_done, 1)
                bank_free(pe, it, (3, remg_ready, 1, 1), (2, vrows_ready, 1, 1))
                if isinstance(it, int) and it == 1:
                    pe.wait_ge(attn_w_ready, 1)
                if isinstance(it, int) and it == 2:
                    pe.wait_ge(wT_ready, 4)
                for t in range(T):
                    last = mm(WB[3][:, t * D:(t + 1) * D], hT[:, t * P:(t + 1) * P], wv[:], start=True, stop=True)
                last.then_inc(v_done, 1)
                bank_free(pe, it, (2, tg_ready, 1, 1))
                if isinstance(it, int) and it == 1:
                    pe.wait_ge(ga_ready, 1)
                    pe.wait_ge(gate_w_ready, 2)
                for k in range(2):
                    last = mm(WB[2][:, k * S:(k + 1) * S], gate_w[:, k, :], hT[:], start=True, stop=True)
                last.then_inc(gates_done, 1)

            def scores(it):
                b = it - 1
                pe.wait_ge(qt_ready, 2 * (b + 1))
                pe.wait_ge(kbd_loaded, N_KBD * (b + 1))
                if isinstance(it, int) and it == 1:
                    pe.wait_ge(masks_loaded, 16 * 4)
                users = [((0, hT_ready, 1, 1), (4, h2T_ready, 1, 1)), ((4, hid_summed, 1, 1), (2, pt_copied, 4, 2)),
                         ((2, a_ready, 1, 1),), ((2, pt_copied, 4, 4),)]
                for k in range(4):
                    t, hh = divmod(k, 2)
                    bank_free(pe, it, *users[k])
                    for q in range(BT):
                        blk = BT * t + q
                        last = mm(SB[k][W * q:W * q + W, :].rearrange("p (h j) -> p h j", h=8),
                                  QT[hh][:, W * blk:W * blk + W],
                                  KBD[:, 8 * hh:8 * hh + 8, W * blk:W * blk + HALF], start=True, stop=True)
                    last.then_inc(s_ready, 1)

            def probs_T(it):
                b = it - 2
                for q in range(4):
                    pe.wait_ge(p_ready, 4 * b + (q + 1))
                    for k in range(4):
                        g2, before = divmod(k, 2)
                        o = ((1 - before) * 8 + 4 * g2) * W
                        last = nc.tensor.transpose(SB[q][:, k * P:(k + 1) * P], Pr[:, q, o:o + P], ident[:])
                    last.then_inc(pt_done, 1)

            def latent_T(it):
                b = it - 2
                pe.wait_ge(pl_ready, 2 * (b + 1))
                bank_free(pe, it, (1, qt_ready, 2, 2))
                for g in range(LG):
                    nc.tensor.transpose(WB[0][:, g * P:(g + 1) * P], PlA[:, 0, g * P:(g + 1) * P], ident[:])
                for g in range(LG):
                    last = nc.tensor.transpose(WB[0][:, (2 + g) * P:(3 + g) * P], PlB[:, 0, g * P:(g + 1) * P], ident[:])
                last.then_inc(lpt_done, 1)
                bank_free(pe, it, (1, gq_ready, 2, 2))
                for g in range(LG):
                    last = nc.tensor.transpose(WB[1][:, g * P:(g + 1) * P], PlB[:, 1, g * P:(g + 1) * P], ident[:])
                last.then_inc(lpt_done, 1)

            def values(it):
                b = it - 2
                pe.wait_ge(pt_copied, 4 * (b + 1))
                pe.wait_ge(vbd_loaded, N_VBD * (b + 1))
                for kb in range(NB):
                    for g in range(G):
                        o = g * 2 * S + kb * W
                        if kb < NB - 1:
                            pt = PT[:, o:o + 2 * (S + W)].rearrange("p (k s) -> p k s", k=2)[:, :, 0:W]
                            dst = SB[2][W * g:W * g + W, kb * W:kb * W + HALF].rearrange("p (k s) -> p k s", k=2)
                        else:
                            pt, dst = PT[:, o:o + W], SB[2][W * g:W * g + W, kb * W:kb * W + W]
                        mm(dst, VBD[:, kb].rearrange("p h (d g) -> p g (h d)", g=G)[:, g, :], pt, start=(kb == 0),
                           stop=(kb == NB - 1), skip_group_check=True)
                pe.wait_ge(pts_ready, T * (b + 1))
                for g in range(G):
                    last = mm(SB[2][W * g:W * g + W, S:2 * S], ones_bd[:], PT_sum[:, g, :], start=False, stop=True,
                              skip_group_check=True)
                last.then_inc(pv_done, 1)

            def latent_values(it):
                b = it - 2
                pe.wait_ge(lpt_copied, 2 * (b + 1))
                pe.wait_ge(gvbd_ready, b + 1)
                for den in range(2):
                    for k in range(2):
                        for t in range(k, T):
                            for g in range(LG):
                                q = (LG * t + g) * W
                                last = mm(WB[0][q:q + W, den * P:(den + 1) * P], ones_bd[:] if den else GVBD[:, k, g, :],
                                          PL[:, g, (t + k) * P:(t + k + 1) * P], start=(den == 0 and k == 0),
                                          stop=(k == t), skip_group_check=True)
                last.then_inc(lpv_done, 1)

            def latent_value_rows(it):
                bank_free(pe, it, (2, lpt_copied, 2, 2), (1, gq_ready, 2, 2))
                wgv_h = wgv[:].rearrange("p (g h d) -> p g h d", g=LG, h=4)
                for k in range(2):
                    for h in range(4):
                        last = mm(WB[1][W * h:W * h + W, k * 16:(k + 1) * 16].rearrange("p (g d) -> p g d", g=LG),
                                  hpT[:, k * W:(k + 1) * W], wgv_h[:, :, h, :], start=True, stop=True)
                last.then_inc(gv_done, 1)

            def latent_scores(it):
                b = it - 1
                pe.wait_ge(gq_ready, 2 * (b + 1))
                pe.wait_ge(gkbd_ready, b + 1)
                for t, m in ((0, W), (1, NL)):
                    if t == 0:
                        pe.wait_ge(gvbd_ready, b + 1)
                    else:
                        bank_free(pe, it, (2, remn_ready, 1, 1), (1, qt_ready, 2, 2))
                    mm(WB[1 - t][:, 0:8 * m].rearrange("p (h j) -> p h j", h=8), GQT[:, t * P:(t + 1) * P],
                       GKBD[:, :, 0:m], start=True, stop=True).then_inc(ls_ready, 1)

            def step(it):
                if has(it, 1):
                    projections(it)
                if has(it, 2):
                    latent_T(it)
                    probs_T(it)
                    latent_values(it)
                if has(it, 1):
                    latent_value_rows(it)
                if has(it, 3):
                    b = it - 3
                    pe.wait_ge(att_ready, b + 1)
                    bank_free(pe, it, (1, vrows_ready, 1, 1))
                    for t in range(T):
                        last = mm(WB[3][:, t * P:(t + 1) * P], attT[:, t * P:(t + 1) * P], w_out_half[:], start=True,
                                  stop=True)
                    last.then_inc(y_done, 1)
                if has(it, 4):
                    pe.wait_ge(xn_d_s, T * (it - 4 + 1))
                    bank_free(pe, it, (2, pt_copied, 4, 1), (5, h2T_ready, 1, 1))
                    for t in range(T):
                        last = nc.tensor.transpose(SB[0][:, t * P:(t + 1) * P], xn_d[:, t, :], ident[:])
                    last.then_inc(x2T_done, 1)
                if has(it, 2):
                    values(it)
                    pe.wait_ge(remn_ready, it - 2 + 1)
                    bank_free(pe, it, (3, yga_ready, 1, 1), (1, vrows_ready, 1, 1))
                    for t in range(T):
                        last = mm(WB[3][:, t * P:(t + 1) * P], r_out[:, t, :], rem_n[:], start=True, stop=True)
                    last.then_inc(rem_done, 1)
                if isinstance(it, int) and it == B + 3:
                    for m in range(2, 4):
                        mix(0, m)
                if has(it, 4):
                    b = it - 4
                    pe.wait_ge(h2T_ready, b + 1)
                    bank_free(pe, it, (2, pt_copied, 4, 2), (5, hid_summed, 1, 1))
                    mm(SB[1][:, 0:S], gate_w1T[:], h2T[:, bass.ds(b * S, S)], start=True, stop=True
                       ).then_inc(hid_done, 1)
                if has(it, 0):
                    pe.wait_ge(xn_a_s, T * (it + 1))
                    bank_free(pe, it, (4, h2T_ready, 1, 1), (2, pt_copied, 4, 1), (1, hT_ready, 1, 1))
                    for t in range(T):
                        last = nc.tensor.transpose(SB[0][:, t * P:(t + 1) * P], xn_a[:, t, :], ident[:])
                    last.then_inc(xT_done, 1)
                if has(it, 1):
                    latent_scores(it)
                    scores(it)

            def experts(g0, g1, ready):
                cols = slice(g0 * GB, g1 * GB)
                n_b = (g1 - g0) * GB
                pe.wait_ge(hid_summed, g1 * GB)
                bank = WB[2] if g0 == 0 else SB[0]
                mm(bank[0:E, 0:n_b], gate_w2T[:], hsum[:, cols], start=True, stop=True).then_inc(g_done, 1)
                if g1 == NG:
                    ffn1(0, 0)
                pe.wait_ge(g_ready, ready + 1)
                rows, biases = (WB[2], SB[3]) if g0 == 0 else (SB[1], SB[2])
                mm(rows[:, 0:n_b], e_rows[:].rearrange("e k j -> e (k j)"), gT[:, cols], start=True, stop=True
                   ).then_inc(g_done, 1)
                for c in range(FC):
                    mm(biases[:, c * n_b:(c + 1) * n_b], tb1[:, c * P:(c + 1) * P], gT[:, cols], start=True, stop=True)
                mm(biases[:, FC * n_b:(FC + 1) * n_b], tb2[:], gT[:, cols], start=True, stop=True).then_inc(g_done, 1)

            def after(it):
                if it == B + 1:
                    pe.wait_ge(tg_ready, B)
                    experts(0, 1, 0)
                if it == B + 2:
                    pe.wait_ge(tw_loaded, N_TW)
                    pe.wait_ge(g_ready, N_G0)
                    pe.wait_ge(yga_ready, B)
                    for m in range(2):
                        mix(0, m)
                if it == B + 3:
                    for m in range(4, 8):
                        pe.wait_ge(mixed, m - 3)
                        mix(0, m)
                    experts(1, NG, N_G0)
                    ffn1(0, 1)
                    pe.wait_ge(g_ready, N_G)
                if it == 0:
                    pe.wait_ge(attn_loaded, N_ATTN)
                    nc.tensor.transpose(SB[1][:, 0:D], wq[:], ident[:]).then_inc(wqT_done, 1)
                    pe.wait_ge(wqT_ready, 1)
                    pe.wait_ge(attn_w_ready, 1)
                    mm(SB[2][:, 0:2 * H], wqT, gate_cols[:, 0:2 * H], start=True, stop=True).then_inc(gate_w_done, 1)
                if it == 1:
                    pe.wait_ge(w_loaded, N_W)
                    pe.wait_ge(vrows_ready, 1)
                    for c in range(FC):
                        last = nc.tensor.transpose(WB[3][:, c * P:(c + 1) * P], W1[:, c, :], ident[:])
                    last.then_inc(wT_done, 1)
                    pe.wait_ge(wT_ready, 1)
                    for c in range(FC):
                        last = nc.tensor.transpose(WB[3][:, c * P:(c + 1) * P], W2[:, c * P:(c + 1) * P], ident[:])
                    last.then_inc(wT_done, 1)
                    pe.wait_ge(wT_ready, 2)
                    nc.tensor.transpose(WB[3][:, 0:P], gate_w1, ident[:])
                    nc.tensor.transpose(WB[3][:, P:P + E], gate_w2, ident[0:E, 0:E]).then_inc(wT_done, 1)

            pipeline(pe, step, after)

            def group(g, last):
                for m in range(8, 16):
                    if m >= 12:
                        pe.wait_ge(mixed, g * 16 + (m - 3))
                    mix(g, m)
                for j in range(GB):
                    ffn2(g, j)
                    if j + 2 < GB:
                        ffn1(g, j + 2)
                    if not last and j == GB - 2:
                        for m in range(4):
                            if m % 2 == 0:
                                pe.wait_ge(gelu_done, g * (FC * GB) + FC * (GB - 1 + m // 2))
                            mix(g + 1, m)
                    if not last and j == GB - 1:
                        for m in range(4, 8):
                            pe.wait_ge(mixed, g * 16 + (16 + m - 3))
                            mix(g + 1, m)
                    if j >= 1:
                        final_T(g, j - 1)
                final_T(g, GB - 1)
                if not last:
                    ffn1(g + 1, 0)
                    ffn1(g + 1, 1)
                    pe.wait_ge(o_ready, (g + 1) * GB)

            with pe.Fori(0, NG - 1) as g:
                group(g, False)
            group(NG - 1, True)


_NAMES = ["L0_attn_x", "L0_attn_wq", "L0_attn_wk", "L0_attn_wv", "L0_attn_wgq", "L0_attn_wgk", "L0_attn_wgv",
          "L0_attn_r_out_w", "L0_attn_gate_local_w", "L0_attn_gate_remote_w", "L0_attn_w_out", "L0_ffn_gate_w1",
          "L0_ffn_gate_b1", "L0_ffn_gate_w2", "L0_ffn_gate_b2", "L0_ffn_W1", "L0_ffn_b1", "L0_ffn_W2", "L0_ffn_b2",
          "L0_ffn_TW1", "L0_ffn_Tb1", "L0_ffn_TW2", "L0_ffn_Tb2", "L0_c", "L0_wmod"]


def kernel(**inputs):
    import concourse.bacc as bacc
    from concourse.bass_utils import run_bass_kernel_spmd

    nc = bacc.Bacc("TRN2", target_bir_lowering=False, num_devices=1)
    arrays, ins = {}, {}
    for name in _NAMES:
        a = np.ascontiguousarray(inputs[name])
        arrays[f"in_{name}"] = a
        ins[name] = nc.dram_tensor(f"in_{name}", a.shape, mybir.dt.from_np(a.dtype), kind="ExternalInput").ap()
    x = arrays["in_L0_attn_x"]
    out = nc.dram_tensor("out_x", x.shape, mybir.dt.from_np(x.dtype), kind="ExternalOutput").ap()
    adaln_block(nc, ins, out)
    r = run_bass_kernel_spmd(nc, [arrays], core_ids=[0])
    return r.results[0]["out_x"]
```
